# Optimizing a Trainium2 kernel written in Bass

```python
import numpy as np
import jax
import jax.numpy as jnp

def _softmax(x, axis=-1):
    return jax.nn.softmax(x, axis=axis)

def _gelu(x):
    return jax.nn.gelu(x, approximate=True)

def _silu(x):
    return jax.nn.silu(x)

def _sigmoid(x):
    return jax.nn.sigmoid(x)

def _layernorm(x, axis=-1, eps=1e-05):
    m = jnp.mean(x, axis=axis, keepdims=True)
    v = jnp.var(x, axis=axis, keepdims=True)
    return (x - m) / jnp.sqrt(v + eps)

def _scatter_add(tgt, idx, src, axis=0):
    return tgt.at[idx].add(src)

def _segment_sum(src, seg, n):
    return jax.ops.segment_sum(src, seg, n)
kernel_name = 'mk_seq_preln_d1_jaxref_r8_5503c7'

def setup_inputs(seed: int=0):
    np.random.seed(seed)
    _w = jnp.asarray

    def _L0_attn_setup():
        import jax, jax.numpy as jnp
        import numpy as np
        import math
        B, S, E, H = (2, 256, 256, 16)
        HD = E // H // 2
        DEPTH = 12
        LAMBDA_INIT = 0.8 - 0.6 * math.exp(-0.3 * DEPTH)
        EPS = 1e-05

        def _rope_interleaved(x, cos, sin):
            xe, xo = (x[..., 0::2], x[..., 1::2])
            c = cos[None, :, None, :]
            s = sin[None, :, None, :]
            oe = xe * c - xo * s
            oo = xe * s + xo * c
            return jnp.stack([oe, oo], axis=-1).reshape(x.shape)
        key = jax.random.key(seed)
        ks = jax.random.split(key, 10)
        sc = 0.02
        return {'x': jax.random.normal(ks[0], (B, S, E), jnp.float32), 'Wq': jax.random.normal(ks[1], (E, E), jnp.float32) * sc, 'Wk': jax.random.normal(ks[2], (E, E), jnp.float32) * sc, 'Wv': jax.random.normal(ks[3], (E, E), jnp.float32) * sc, 'Wo': jax.random.normal(ks[4], (E, E), jnp.float32) * sc, 'lambda_q1': jax.random.normal(ks[5], (HD,), jnp.float32) * 0.1, 'lambda_k1': jax.random.normal(ks[6], (HD,), jnp.float32) * 0.1, 'lambda_q2': jax.random.normal(ks[7], (HD,), jnp.float32) * 0.1, 'lambda_k2': jax.random.normal(ks[8], (HD,), jnp.float32) * 0.1, 'gamma': jnp.ones((2 * HD,), jnp.float32)}
    _L0_attn_in = _L0_attn_setup()

    def _L0_ffn_setup():
        import jax, jax.numpy as jnp
        import numpy as np
        D_MODEL = 256
        HIDDEN = int(2 * D_MODEL * 4 / 3)

        def ternary_quant(w):
            s = jnp.mean(jnp.abs(w))
            q = jnp.clip(jnp.round(w / s), -1.0, 1.0) * s
            return w + jax.lax.stop_gradient(q - w)
        key = jax.random.key(seed)
        k0, k1, k2, k3 = jax.random.split(key, 4)
        x = jax.random.normal(k0, (4, 512, D_MODEL), dtype=jnp.float32)
        std_in = 1.0 / np.sqrt(D_MODEL)
        std_h = 1.0 / np.sqrt(HIDDEN)
        w1 = jax.random.uniform(k1, (HIDDEN, D_MODEL), jnp.float32, -std_in, std_in)
        w3 = jax.random.uniform(k2, (HIDDEN, D_MODEL), jnp.float32, -std_in, std_in)
        w2 = jax.random.uniform(k3, (D_MODEL, HIDDEN), jnp.float32, -std_h, std_h)
        return {'x': x, 'w1': w1, 'w3': w3, 'w2': w2}
    _L0_ffn_in = _L0_ffn_setup()
    _d = {'L0_attn_x': _L0_attn_in['x'], 'L0_attn_Wq': _L0_attn_in['Wq'], 'L0_attn_Wk': _L0_attn_in['Wk'], 'L0_attn_Wv': _L0_attn_in['Wv'], 'L0_attn_Wo': _L0_attn_in['Wo'], 'L0_attn_lambda_q1': _L0_attn_in['lambda_q1'], 'L0_attn_lambda_k1': _L0_attn_in['lambda_k1'], 'L0_attn_lambda_q2': _L0_attn_in['lambda_q2'], 'L0_attn_lambda_k2': _L0_attn_in['lambda_k2'], 'L0_attn_gamma': _L0_attn_in['gamma'], 'L0_ffn_w1': _L0_ffn_in['w1'], 'L0_ffn_w3': _L0_ffn_in['w3'], 'L0_ffn_w2': _L0_ffn_in['w2']}
    _x0 = _d['L0_attn_x']
    _d['L0_attn_x'] = jax.random.normal(jax.random.fold_in(jax.random.key(seed), 1), (8, 512, 256), dtype=_x0.dtype)
    del _x0
    return _d

def reference(L0_attn_x, L0_attn_Wq, L0_attn_Wk, L0_attn_Wv, L0_attn_Wo, L0_attn_lambda_q1, L0_attn_lambda_k1, L0_attn_lambda_q2, L0_attn_lambda_k2, L0_attn_gamma, L0_ffn_w1, L0_ffn_w3, L0_ffn_w2):

    def _L0_attn_ref(x, Wq, Wk, Wv, Wo, lambda_q1, lambda_k1, lambda_q2, lambda_k2, gamma):
        import jax, jax.numpy as jnp
        import numpy as np
        import math
        B, S, E, H = (2, 256, 256, 16)
        HD = E // H // 2
        DEPTH = 12
        LAMBDA_INIT = 0.8 - 0.6 * math.exp(-0.3 * DEPTH)
        EPS = 1e-05

        def _rope_interleaved(x, cos, sin):
            xe, xo = (x[..., 0::2], x[..., 1::2])
            c = cos[None, :, None, :]
            s = sin[None, :, None, :]
            oe = xe * c - xo * s
            oo = xe * s + xo * c
            return jnp.stack([oe, oo], axis=-1).reshape(x.shape)
        b, t, _ = x.shape
        angle = 1.0 / 1250 ** jnp.linspace(0.0, 1.0, HD // 2, dtype=jnp.float32)
        freqs = jnp.arange(t, dtype=jnp.float32)[:, None] * angle
        cos, sin = (jnp.cos(freqs), jnp.sin(freqs))
        q = (x @ Wq.T).reshape(b, t, 2 * H, HD)
        k = (x @ Wk.T).reshape(b, t, 2 * H, HD)
        v = (x @ Wv.T).reshape(b, t, H, 2 * HD)
        q = _rope_interleaved(q, cos, sin)
        k = _rope_interleaved(k, cos, sin)
        q = q.reshape(b, t, H, 2, HD)
        k = k.reshape(b, t, H, 2, HD)
        q1, q2 = (q[:, :, :, 0], q[:, :, :, 1])
        k1, k2 = (k[:, :, :, 0], k[:, :, :, 1])
        scale = HD ** (-0.5)
        s1 = jnp.einsum('bthd,bshd->bhts', q1, k1) * scale
        p1 = jax.nn.softmax(s1, axis=-1)
        o1 = jnp.einsum('bhts,bshd->bthd', p1, v)
        s2 = jnp.einsum('bthd,bshd->bhts', q2, k2) * scale
        p2 = jax.nn.softmax(s2, axis=-1)
        o2 = jnp.einsum('bhts,bshd->bthd', p2, v)
        lam1 = jnp.exp(jnp.sum(lambda_q1 * lambda_k1))
        lam2 = jnp.exp(jnp.sum(lambda_q2 * lambda_k2))
        lam = lam1 - lam2 + LAMBDA_INIT
        attn = o1 - lam * o2
        rms = jax.lax.rsqrt(jnp.mean(attn * attn, axis=-1, keepdims=True) + EPS)
        attn = attn * rms * gamma
        attn = attn * (1.0 - LAMBDA_INIT)
        attn = attn.reshape(b, t, H * 2 * HD)
        return attn @ Wo.T

    def _L0_ffn_ref(x, w1, w3, w2):
        import jax, jax.numpy as jnp
        import numpy as np
        D_MODEL = 256
        HIDDEN = int(2 * D_MODEL * 4 / 3)

        def ternary_quant(w):
            s = jnp.mean(jnp.abs(w))
            q = jnp.clip(jnp.round(w / s), -1.0, 1.0) * s
            return w + jax.lax.stop_gradient(q - w)
        w1q = ternary_quant(w1)
        w3q = ternary_quant(w3)
        w2q = ternary_quant(w2)
        h1 = jnp.einsum('bsd,hd->bsh', x, w1q)
        h3 = jnp.einsum('bsd,hd->bsh', x, w3q)
        g = jax.nn.silu(h1) * h3
        return jnp.einsum('bsh,dh->bsd', g, w2q)
    x = L0_attn_x
    x = x + _L0_attn_ref(_layernorm(x, axis=-1), L0_attn_Wq, L0_attn_Wk, L0_attn_Wv, L0_attn_Wo, L0_attn_lambda_q1, L0_attn_lambda_k1, L0_attn_lambda_q2, L0_attn_lambda_k2, L0_attn_gamma)
    x = x + _L0_ffn_ref(_layernorm(x, axis=-1), L0_ffn_w1, L0_ffn_w3, L0_ffn_w2)
    return x

_drawn_inputs = setup_inputs


def setup_inputs(seed=0):
    import zlib

    import numpy as np

    out = dict(_drawn_inputs(seed))
    spreads = {'L0_attn_gamma': (1.0, 0.6)}
    factors = {'L0_attn_lambda_q1': 200.0,
     'L0_attn_lambda_k1': 8.0,
     'L0_attn_lambda_q2': 63.656,
     'L0_attn_lambda_k2': 58.368,
     'L0_attn_Wq': 4.146,
     'L0_attn_Wk': 4.087}
    for name, (base, spread) in spreads.items():
        noise = np.random.default_rng([zlib.crc32(name.encode()), seed]).standard_normal(out[name].shape)
        drawn = base * np.exp(spread * noise) if base else spread * noise
        out[name] = jnp.asarray(drawn.astype(out[name].dtype))
    for name, factor in factors.items():
        out[name] = (out[name] * factor).astype(out[name].dtype)
    return out
```

```python
from contextlib import ExitStack

import numpy as np

import concourse.bass as bass
from concourse import mybir

F32, BF16, F16 = mybir.dt.float32, mybir.dt.bfloat16, mybir.dt.float16
ALU = mybir.AluOpType
ACT = mybir.ActivationFunctionType
AX = mybir.AxisListType

B, T, E = 8, 512, 256
H, HD = 16, 8
VD = 2 * HD
P = 128
NT = T // P
EC = E // P
HIDDEN = int(2 * E * 4 / 3)
HB = 114
NB = -(-HIDDEN // HB)
HPAD = HB * NB
QUADS = 2 * H // 4
SLOTS = 8
ROWS = 64
BLOCK = ROWS // (HD // 2)
SHIFT_ROW = 12
LAMBDA_INIT = 0.8 - 0.6 * float(np.exp(-0.3 * 12))
EPS = 1e-5
SQUARE_MAX = 2.0 ** 64 * (1 - 2.0 ** -20)
MEAN_MAX = 2.0 ** 124 * (1 - 2.0 ** -18)
SCALE = HD ** -0.5
Q_BLOCKS = ((0, 1, 3), (3, 2, 2), (4, 1, 1))
K_BLOCKS = ((2, 1, 3), (0, 5, 2), (1, 1, 1))
PV_SLOTS = (0, 2, 4, 6)
S_BANKS = [n % 3 for n in range(15)] + [1]

JOBS = {}


def _place(t, *job):
    JOBS.setdefault(t, []).append(job)


OP_AT = (21, 23)
LN1_AT = (1, 3, 4, 5)
LN2_AT = (23, 26, 27, 29)
ROPE_AT = {13: (0, 6), 18: (6, 11), 20: (11, 16), 25: (16, 18), 27: (18, 20)}
CAST_AT = {18: (0, 1), 21: (2, 3), 24: (4, 5), 26: (6, 7)}
for _c in range(EC):
    _place(7 + _c, "pre", "X1T", _c)
for _j, _t in enumerate((9, 11, 13, 15)):
    _place(_t, "pre", "QK", _j)
for _h in range(2):
    _place(62 + _h, "pre", "V", _h)
for _k in range(QUADS):
    _place(8 * _k + 1, "att", "OT", _k)
    _place(8 * _k + 2, "att", "MT", _k)
for _n in range(2):
    _place(18 + _n, "post", "AT", _n)
    _place(OP_AT[_n], "post", "OP", _n)
    _place(31 + 2 * _n, "post", "X2T", _n)
    _place((59, 61)[_n], "post", "DN", _n)
for _m in range(NB):
    _place((35, 38, 42, 46, 50, 54)[_m], "post", "A", _m)
    _place((37, 40, 44, 48, 52, 56)[_m], "post", "B", _m)
ORDER = [job for t in sorted(JOBS) for job in JOBS[t]]
BANK = {job[1:]: n % 2 for n, job in enumerate(ORDER)}
PRE_USED = {("X1T", c): c for c in range(EC)} | {("QK", j): 2 + j for j in range(4)} | {("V", h): 6 + h for h in range(2)}
POST_USED = ({("AT", n): n for n in range(2)} | {("OP", n): 2 + n for n in range(2)} | {("X2T", n): 4 + n for n in range(2)}
             | {("A", m): 6 + 2 * m for m in range(NB)} | {("B", m): 7 + 2 * m for m in range(NB)}
             | {("DN", n): 6 + 2 * NB + n for n in range(2)})
NPRE, NPOST = len(PRE_USED), len(POST_USED)


def job_batch(cat, name, k, i):
    if cat == "pre":
        return i + 1, k
    if cat == "post":
        return i - 1, k
    if name == "OT":
        return (i, k - 2) if k >= 2 else (i - 1, k + 6)
    return (i, k + 1) if k < 7 else (i + 1, 0)


def wait(eng, sem, value):
    if not isinstance(value, int) or value > 0:
        eng.wait_ge(sem, value)


def build(nc, x, wqk, wv, wo, w1, w3, w2, rope, ident_in, pads, lam_in, gamma_in, out):
    with ExitStack() as ctx:
        def sb(name, shape, dt):
            return ctx.enter_context(nc.sbuf_tensor(name, shape, dt))

        def pb(name, shape, dt):
            return ctx.enter_context(nc.psum_tensor(name, shape, dt))

        def sem(name):
            return ctx.enter_context(nc.semaphore(name))

        scratch = [nc.dram_tensor(f"stack_{s}", [2 * H, ROWS, T], BF16).ap() for s in "qk"]

        ident = sb("ident", [P, P], F32)
        identb = sb("identb", [P, P], BF16)
        ones = sb("ones", [P, P], F32)
        minus_half = sb("minus_half", [P, 8], F32)
        wqk_sb = sb("wqk_sb", [P, EC, 4, P], F32)
        wv_sb = sb("wv_sb", [P, EC, E], F32)
        wo_sb = sb("wo_sb", [P, EC, E], F32)
        t13 = sb("t13", [P, 2, EC, HPAD], F16)
        t2 = sb("t2", [HB, NB, E], F16)
        cos_sin = sb("cos_sin", [P, 2, T], F32)
        gcol = sb("gcol", [P, 1], F32)
        lam_v = sb("lam_v", [P, 4, HD], F32)
        lam_p = sb("lam_p", [P, 2, HD], F32)
        lam_s = sb("lam_s", [P, 2], F32)
        lam_e = sb("lam_e", [P, 2], F32)
        neg_lam = sb("neg_lam", [P, 1], F32)
        abs_sums = sb("abs_sums", [P, 3], F32)
        scales = sb("scales", [P, 3], F32)
        half = sb("half", [P, 3], F32)
        neg_half = sb("neg_half", [P, 3], F32)
        s13 = sb("s13", [P, 1], F32)
        out_scale = sb("out_scale", [P, 1], F32)
        q_stack = sb("q_stack", [P, QUADS, 2, T], BF16)
        k_stack = sb("k_stack", [P, QUADS, 2, T], BF16)
        probs = sb("probs", [P, 2, NT, 4, T], F32)
        v_next = sb("v_next", [P, NT, H, VD + 1], F32)
        v_sb = sb("v_sb", [P, NT, H, VD + 1], F32)
        x_pre = sb("x_pre", [P, NT, E], F32)
        x_res = sb("x_res", [P, NT, E], F32)
        x1n = sb("x1n", [P, NT, E], F32)
        g = x1n[0:HB].rearrange("p (a n) e -> p a (n e)", a=2)
        xhT = sb("xhT", [P, EC, T], F32)
        raw = sb("raw", [P, 4, T], F32)
        roped_even = sb("roped_even", [P, 2, T], F32)
        rope_tmp = sb("rope_tmp", [P, T], F32)
        parts = sb("parts", [P, 2, 3, 2, T], BF16)
        row_max = sb("row_max", [P, 2, NT, 2, 2], F32)
        max_parts = sb("max_parts", [P, NT, 2, 2, 2], BF16)
        max_rows = sb("max_rows", [8, 2, T], BF16)
        o_sb = sb("o_sb", [P, T], F32)
        o_recip = sb("o_recip", [P, NT, 4], F32)
        o_scaled = sb("o_scaled", [P, NT, 4, VD], F32)
        o_diff = sb("o_diff", [P, NT, 2, VD], F32)
        o_sq = sb("o_sq", [P, NT, 2, VD], F32)
        o_ss = sb("o_ss", [P, 8], F32)
        o_ms = sb("o_ms", [P, 8], F32)
        o_rms = sb("o_rms", [P, 8], F32)
        o_rms_in = sb("o_rms_in", [P, 8], F32)
        attn = sb("attn", [P, NT, E], F32)
        attnT = sb("attnT", [P, EC, T], F32)
        x2 = sb("x2", [P, NT, E], F32)
        x2n = attnT[:, :, :].rearrange("p c (n e) -> p (c n) e", e=E)
        stats = [sb(f"stats{n}", [P, NT, 6], F32) for n in (1, 2)]
        mean_var = [sb(f"mean_var{n}", [P, NT, 2], F32) for n in (1, 2)]
        var_eps = [sb(f"var_eps{n}", [P, NT], F32) for n in (1, 2)]
        rstd = [sb(f"rstd{n}", [P, NT], F32) for n in (1, 2)]
        x2T = sb("x2T", [P, 2, EC, T], F16)
        th = x_res[0:HB].rearrange("p (a n) e -> p a (n e)", a=2)
        gate = sb("gate", [HB, T], F32)
        gT = sb("gT", [HB, 2, NB, T], F16)

        late = probs[:, 1].rearrange("p c s t -> p (c s t)")
        w13_raw = late[:, 0:2 * EC * HPAD].rearrange("p (w c h) -> p w c h", w=2, c=EC)
        w2_raw = late[0:HB, 2 * EC * HPAD:2 * EC * HPAD + NB * E].rearrange("p (m e) -> p m e", m=NB)
        below = late[:, 2 * EC * HPAD + NB * E:2 * EC * HPAD + NB * E + NB * E]

        st_bank = [pb(f"st{n}", [P, T], F32) for n in range(2)]
        s_bank = [pb(f"s{n}", [P, T], F32) for n in range(3)]
        o_bank = pb("o_bank", [P, T], F32)
        d_bank = [pb(f"d{n}", [P, T], F32) for n in range(2)]

        ld_x = sem("ld_x")
        ld_xres = sem("ld_xres")
        ld_w = {n: sem(f"ld_{n}") for n in ("ident", "qk", "rope", "vo", "tern", "small", "pads")}
        scr_written = sem("scr_written")
        stack_loaded = [sem(f"stack_loaded{q}") for q in range(QUADS)]
        shift_loaded = [sem(f"shift_loaded{n}") for n in range(2)]
        out_stored = sem("out_stored")
        consts = sem("consts")
        abs_done = sem("abs_done")
        scale_ready = sem("scale_ready")
        setup = sem("setup")
        lam_sum = sem("lam_sum")
        lam_exp = sem("lam_exp")
        lam_done = sem("lam_done")
        wo_scaled = sem("wo_scaled")
        ternary = sem("ternary")
        st_ready = sem("st_ready")
        s_ready = sem("s_ready")
        pv_done = sem("pv_done")
        pre_ready, mt_ready, ot_ready, post_ready = (sem(n) for n in ("pre_ready", "mt_ready", "ot_ready", "post_ready"))
        pre_used, mt_used, ot_used, post_used = (sem(n) for n in ("pre_used", "mt_used", "ot_used", "post_used"))
        exp_done = sem("exp_done")
        v_ready = sem("v_ready")
        o_copied = sem("o_copied")
        cast_done = sem("cast_done")
        x2h_done = sem("x2h_done")
        tanh_done = sem("tanh_done")
        ghi_done = sem("ghi_done")
        s_used = sem("s_used")
        max_hi = sem("max_hi")
        max_split = sem("max_split")
        o_step = sem("o_step")
        o_rms_done = sem("o_rms_done")
        o_masked = sem("o_masked")
        o_norm = sem("o_norm")
        ln_step = [sem(f"ln_step{n}") for n in (1, 2)]
        ln_rstd = [sem(f"ln_rstd{n}") for n in (1, 2)]
        ln_out = [sem(f"ln_out{n}") for n in (1, 2)]
        rope_step = sem("rope_step")
        glo_done = sem("glo_done")

        QK_READY, LOOP = 2, (1, B - 1)
        CASTS, ROPE = 8, 20

        def job_used(name, n, b):
            if name == "OT":
                return ot_used, 8 * b + n + 1
            if name == "MT":
                return mt_used, 8 * b + n + 1
            if (name, n) in PRE_USED:
                return pre_used, NPRE * b + PRE_USED[name, n] + 1
            return post_used, NPOST * b + POST_USED[name, n] + 1

        def runs(cat, name, k, att, pre, post):
            if cat == "pre":
                return pre
            if cat == "post":
                return post
            if name == "OT":
                return att if k >= 2 else post
            return att if k < 7 else pre

        x_v = x.rearrange("b (n p) e -> b p n e", p=P)
        out_v = out.rearrange("b (n p) e -> b p n e", p=P)
        block = ctx.enter_context(nc.Block())

        @block.sync
        def _(sp):
            def load_x(b, dst, done):
                sp.dma_start(dst[:, :, :], x_v[b]).then_inc(done, 16)

            def write_parts(side, b):
                if side == 0:
                    for q in range(QUADS):
                        wait(sp, stack_loaded[q], 32 * b)
                sp.wait_ge(rope_step, ROPE * b + (16 if side == 0 else 20))
                rows = scratch[side].rearrange("h (f c a) t -> (h f) c (a t)", c=BLOCK // 2, a=2)
                for part, (first, step, count) in enumerate((Q_BLOCKS, K_BLOCKS)[side]):
                    src = parts[:, side, part].rearrange("p a t -> p (a t)")
                    sp.dma_start(rows[:, first:first + step * (count - 1) + 1:step],
                                 src.unsqueeze(1).to_broadcast([P, count, 2 * T])).then_inc(scr_written, 16)

            def load_stack(b, q):
                if q == 0:
                    sp.wait_ge(scr_written, 96 * b + 96)
                if q == QUADS - 1:
                    wait(sp, st_ready, 128 * b)
                for side, dst in enumerate((q_stack, k_stack)):
                    src = scratch[side].rearrange("(g a j) r t -> g (j r) a t", a=2, j=2)
                    sp.dma_start(dst[:, q, :, :], src[q]).then_inc(stack_loaded[q], 16)

            def load_shift(b, q):
                sp.wait_ge(mt_used, 8 * b + q + 1)
                for pair in range(2):
                    for j in range(2):
                        r = 4 * pair + 2 * j
                        sp.dma_start(q_stack[64 * j + SHIFT_ROW:64 * j + SHIFT_ROW + 2, q, pair, :],
                                     max_rows[r:r + 2, q % 2, :]).then_inc(shift_loaded[q % 2], 16)

            def iteration(i, att, pre, post):
                if pre and not post:
                    sp.wait_ge(ln_out[0], 4)
                if not att:
                    sp.wait_ge(post_used, NPOST * (i - 1))
                if att and post:
                    load_stack(i, 7)
                if pre:
                    load_x(i + 1, x_pre, ld_x)
                if post:
                    load_x(i - 1, x_res, ld_xres)
                for k in range(QUADS):
                    if att and k < 7:
                        load_shift(i, k + 1)
                    if pre:
                        if k == 2:
                            write_parts(0, i + 1)
                        if k == 3:
                            write_parts(1, i + 1)
                        if k == 4:
                            for q in range(4):
                                load_stack(i + 1, q)
                        if k == 5:
                            load_stack(i + 1, 4)
                        if k == 6:
                            load_stack(i + 1, 5)
                        if k == 7:
                            load_shift(i + 1, 0)
                if post:
                    sp.wait_ge(post_used, NPOST * i)
                if pre:
                    load_stack(i + 1, 6)
                if post:
                    sp.dma_start(out_v[i - 1], x2[:, :, :]).then_inc(out_stored, 16)

            load_x(0, x_pre, ld_x)
            sp.dma_start(ident[:, :], ident_in).then_inc(ld_w["ident"], 16)
            sp.dma_start(wqk_sb[:, :, :, :], wqk.rearrange("(c p) j m -> p c j m", p=P)).then_inc(ld_w["qk"], 16)
            sp.dma_start(cos_sin[:, :, :], rope.rearrange("a p t -> p a t")).then_inc(ld_w["rope"], 16)
            sp.dma_start(lam_v[:, :, :], lam_in.partition_broadcast(P)).then_inc(ld_w["small"], 16)
            sp.dma_start(gcol[:, :], gamma_in).then_inc(ld_w["small"], 16)
            for w, src in enumerate((w1, w3)):
                sp.dma_start(w13_raw[:, w], src.rearrange("(c p) h -> p c h", p=P)).then_inc(ld_w["tern"], 16)
            sp.dma_start(w2_raw, w2.rearrange("(m p) e -> p m e", p=HB)).then_inc(ld_w["tern"], 16)
            sp.dma_start(wv_sb[:, :, :], wv.rearrange("(c p) e -> p c e", p=P)).then_inc(ld_w["vo"], 16)
            sp.dma_start(wo_sb[:, :, :], wo.rearrange("(c p) e -> p c e", p=P)).then_inc(ld_w["vo"], 16)
            for side in range(2):
                spare = scratch[side].rearrange("h (f r) t -> h f (r t)", r=BLOCK)[:, :, SHIFT_ROW * T:]
                sp.dma_start(spare, pads[side:side + 1].to_broadcast([2 * H, HD // 2, (BLOCK - SHIFT_ROW) * T])
                             ).then_inc(ld_w["pads"], 16)
            write_parts(0, 0)
            write_parts(1, 0)
            sp.wait_ge(ld_w["pads"], 32)
            for q in range(QUADS):
                load_stack(0, q)
            load_shift(0, 0)
            iteration(0, True, True, False)
            with sp.Fori(*LOOP) as i:
                iteration(i, True, True, True)
            iteration(B - 1, True, False, True)
            iteration(B, False, False, True)
            sp.wait_ge(out_stored, 16 * B)

        @block.tensor
        def _(pe):
            last_on_bank = {}

            def take_bank(name, n, b):
                bank = BANK[name, n if name not in ("OT", "MT") else job_slot[name, n]]
                if bank in last_on_bank:
                    s, v = job_used(*last_on_bank[bank])
                    wait(pe, s, v)
                last_on_bank[bank] = (name, n, b)
                return d_bank[bank]

            job_slot = {("OT", q): (q + 2) % 8 for q in range(8)} | {("MT", q): (q - 1) % 8 for q in range(8)}

            def transposed_scores(b, q, m):
                if m == 0:
                    sem_q = shift_loaded[q % 2]
                    pe.wait_ge(sem_q, 256 * b + 64 * (q // 2) + 64)
                chunk, pair = m // 2, m % 2
                for j in range(2):
                    wait(pe, exp_done, 128 * b + 16 * q + 2 * m + j - 1)
                    rows = slice(64 * j, 64 * j + ROWS)
                    pe.matmul(st_bank[j][:, :], k_stack[rows, q, pair, chunk * P:chunk * P + P],
                              q_stack[rows, q, pair, :], start=True, stop=True).then_inc(st_ready, 1)

            def scores(b, q, m):
                if m == 0:
                    pe.wait_ge(stack_loaded[q], 32 * b + 32)
                tile, pair = m // 2, m % 2
                for j in range(2):
                    n = 2 * m + j
                    back = next(d for d in range(1, 17) if S_BANKS[(n - d) % 16] == S_BANKS[n])
                    wait(pe, s_used, 128 * b + 16 * q + n - back + 1)
                    rows = slice(64 * j, 64 * j + ROWS)
                    pe.matmul(s_bank[S_BANKS[n]][:, :], q_stack[rows, q, pair, tile * P:tile * P + P],
                              k_stack[rows, q, pair, :], start=True, stop=True).then_inc(s_ready, 1)

            def values(b, q, c):
                pe.wait_ge(exp_done, 128 * b + 16 * q + 4 * c + 4)
                if q == 0:
                    pe.wait_ge(v_ready, 4 * b + c + 1)
                if c == 0:
                    wait(pe, o_copied, 8 * b + q)
                for slot in range(4):
                    head = 2 * q + slot // 2
                    mm = pe.matmul(o_bank[32 * slot:32 * slot + VD + 1, :], v_sb[:, c, head, :],
                                   probs[:, q % 2, c, slot, :], start=(c == 0), stop=(c == NT - 1))
                mm.then_inc(pv_done, 1)

            def transpose_tiles(d, src, idn):
                for n in range(NT):
                    t = pe.transpose(d[:, n * P:n * P + P], src(n), idn)
                return t

            def dense(name, n, b):
                d = take_bank(name, n, b)
                if name == "X1T":
                    pe.wait_ge(ln_out[0], 4 * b + 4)
                    transpose_tiles(d, lambda t: x1n[:, t, n * P:n * P + P], ident[:, :]).then_inc(pre_ready, 1)
                elif name == "QK":
                    pe.wait_ge(pre_used, NPRE * b + QK_READY)
                    for c in range(EC):
                        mm = pe.matmul(d[:, :], wqk_sb[:, c, n, :], xhT[:, c, :], start=(c == 0), stop=(c == EC - 1))
                    mm.then_inc(pre_ready, 1)
                elif name == "V":
                    for t in range(2 * n, 2 * n + 2):
                        for c in range(EC):
                            mm = pe.matmul(d[:, (t % 2) * E:(t % 2) * E + E], xhT[:, c, t * P:t * P + P],
                                           wv_sb[:, c, :], start=(c == 0), stop=(c == EC - 1))
                    mm.then_inc(pre_ready, 1)
                elif name == "MT":
                    pe.wait_ge(max_split, 8 * b + n + 1)
                    d16 = d[:, :].bitcast(BF16)
                    for t in range(NT):
                        mm = pe.transpose(d16[0:8, t * P:t * P + P],
                                          max_parts[:, t].rearrange("p a j x -> p (a j x)"), identb[:, :])
                    mm.then_inc(mt_ready, 1)
                elif name == "OT":
                    pe.wait_ge(o_copied, 8 * b + n + 1)
                    transpose_tiles(d, lambda t: o_sb[:, t * P:t * P + P], ident[:, :]).then_inc(ot_ready, 1)
                elif name == "AT":
                    pe.wait_ge(o_norm, 8 * b + 8)
                    transpose_tiles(d, lambda t: attn[:, t, n * P:n * P + P], ident[:, :]).then_inc(post_ready, 1)
                elif name == "OP":
                    pe.wait_ge(post_used, NPOST * b + POST_USED["AT", 1] + 1)
                    for t in range(2 * n, 2 * n + 2):
                        for c in range(EC):
                            mm = pe.matmul(d[:, (t % 2) * E:(t % 2) * E + E], attnT[:, c, t * P:t * P + P],
                                           wo_sb[:, c, :], start=(c == 0), stop=(c == EC - 1))
                    mm.then_inc(post_ready, 1)
                elif name == "X2T":
                    pe.wait_ge(ln_out[1], 4 * b + 4)
                    transpose_tiles(d, lambda t: x2n[:, t, n * P:n * P + P], ident[:, :]).then_inc(post_ready, 1)
                elif name in "AB":
                    pe.wait_ge(post_used, NPOST * b + POST_USED["X2T", 1] + 1)
                    for c in range(EC):
                        for part in range(2):
                            mm = pe.matmul(d[0:HB, :], t13[:, "AB".index(name), c, n * HB:n * HB + HB],
                                           x2T[:, part, c, :], start=(c == 0 and part == 0),
                                           stop=(c == EC - 1 and part == 1))
                    mm.then_inc(post_ready, 1)
                elif name == "DN":
                    pe.wait_ge(glo_done, NB * b + NB)
                    for t in range(2 * n, 2 * n + 2):
                        for m in range(NB):
                            for part in range(2):
                                mm = pe.matmul(d[:, (t % 2) * E:(t % 2) * E + E], gT[:, part, m, t * P:t * P + P],
                                               t2[:, m, :], start=(m == 0 and part == 0),
                                               stop=(m == NB - 1 and part == 1))
                    mm.then_inc(post_ready, 1)

            def iteration(i, att, pre, post):
                for t in range(8 * QUADS):
                    k, m = t // 8, t % 8
                    if att:
                        transposed_scores(i, k, m)
                    if k + 2 < QUADS and att:
                        scores(i, k + 2, m)
                    if k + 2 >= QUADS and pre:
                        scores(i + 1, k + 2 - QUADS, m)
                    if m in PV_SLOTS and (att if k else post):
                        values(*((i, k - 1) if k else (i - 1, QUADS - 1)), PV_SLOTS.index(m))
                    for cat, name, n in JOBS.get(t, ()):
                        if runs(cat, name, n, att, pre, post):
                            b, q = job_batch(cat, name, n, i)
                            dense(name, q, b)

            pe.wait_ge(ld_w["ident"], 16)
            pe.wait_ge(consts, 5)
            for c in range(EC):
                dense("X1T", c, 0)
            pe.wait_ge(ld_w["qk"], 16)
            for j in range(4):
                dense("QK", j, 0)
            pe.wait_ge(ld_w["vo"], 32)
            for h in range(2):
                dense("V", h, 0)
            pe.wait_ge(pre_used, NPRE)
            pe.wait_ge(abs_done, 4)
            pe.matmul(d_bank[0][:, 0:3], ones[:, :], abs_sums[:, :], start=True, stop=True).then_inc(scale_ready, 1)
            pe.wait_ge(setup, 1)
            for m in range(SLOTS):
                scores(0, 0, m)
            dense("MT", 0, 0)
            for m in range(SLOTS):
                scores(0, 1, m)
            iteration(0, True, True, False)
            pe.wait_ge(wo_scaled, 2)
            pe.wait_ge(ternary, 3)
            with pe.Fori(*LOOP) as i:
                for h in range(2):
                    last_on_bank[BANK["V", h]] = ("V", h, i)
                iteration(i, True, True, True)
            for h in range(2):
                last_on_bank[BANK["V", h]] = ("V", h, B - 1)
            iteration(B - 1, True, False, True)
            iteration(B, False, False, True)

        @block.scalar
        def _(act):
            def exps(b, q, m):
                chunk, pair = m // 2, m % 2
                for j in range(2):
                    n = 2 * m + j
                    act.wait_ge(st_ready, 128 * b + 16 * q + n + 1)
                    act.activation(probs[:, q % 2, chunk, 2 * pair + j, :], st_bank[j][:, :], ACT.Exp,
                                   scale=SCALE).then_inc(exp_done, 1)

            def copy_x1T(b, c):
                act.wait_ge(pre_ready, NPRE * b + PRE_USED["X1T", c] + 1)
                act.copy(xhT[:, c, :], d_bank[BANK["X1T", c]][:, :]).then_inc(pre_used, 1)

            def copy_raw(b, j):
                act.wait_ge(pre_ready, NPRE * b + PRE_USED["QK", j] + 1)
                wait(act, rope_step, ROPE * b)
                act.copy(raw[:, j, :], d_bank[BANK["QK", j]][:, :]).then_inc(pre_used, 1)

            def copy_v(b, h):
                act.wait_ge(pre_ready, NPRE * b + PRE_USED["V", h] + 1)
                wait(act, v_ready, 4 * b)
                act.copy(v_next[:, 2 * h:2 * h + 2, :, 0:VD],
                         d_bank[BANK["V", h]][:, :].rearrange("p (n h e) -> p n h e", n=2, h=H)).then_inc(pre_used, 1)

            def move_v(b, c):
                act.wait_ge(pre_used, NPRE * b + NPRE)
                wait(act, pv_done, 32 * (b - 1) + 28 + c + 1)
                act.copy(v_sb[:, c], v_next[:, c]).then_inc(v_ready, 1)

            def copy_o(b, q):
                act.wait_ge(pv_done, 32 * b + 4 * q + 4)
                wait(act, ot_ready, 8 * b + q)
                act.copy(o_sb[:, :], o_bank[:, :]).then_inc(o_copied, 1)

            def copy_max_rows(b, q):
                act.wait_ge(mt_ready, 8 * b + q + 1)
                if q >= 2:
                    act.wait_ge(shift_loaded[q % 2], 256 * b + 64 * (q // 2))
                else:
                    wait(act, shift_loaded[q % 2], 256 * b)
                d16 = d_bank[BANK["MT", (q - 1) % 8]][:, :].bitcast(BF16)
                act.copy(max_rows[:, q % 2, :], d16[0:8, 0:T]).then_inc(mt_used, 1)

            def cast_part(b, n):
                side, part, a = n // 4, (n // 2) % 2, n % 2
                src = roped_even[:, side, :] if a == 0 else raw[:, 2 * side + 1, :]
                if n == 0:
                    wait(act, scr_written, 96 * b)
                act.wait_ge(rope_step, ROPE * b + (6, 8, 14, 18)[n // 2])
                act.copy(parts[:, side, part, a, :], src).then_inc(cast_done, 1)

            def copy_attnT(b, c):
                act.wait_ge(post_ready, NPOST * b + POST_USED["AT", c] + 1)
                act.copy(attnT[:, c, :], d_bank[BANK["AT", c]][:, :]).then_inc(post_used, 1)

            def x2_high(b, c):
                act.wait_ge(post_ready, NPOST * b + POST_USED["X2T", c] + 1)
                act.copy(x2T[:, 0, c, :], d_bank[BANK["X2T", c]][:, :]).then_inc(x2h_done, 1)

            def tanh(b, m):
                act.wait_ge(post_ready, NPOST * b + POST_USED["A", m] + 1)
                if m >= 2:
                    act.wait_ge(post_used, NPOST * b + POST_USED["A", m - 2] + 1)
                act.activation(th[:, m % 2, :], d_bank[BANK["A", m]][0:HB, :], ACT.Tanh,
                               scale=half[0:HB, 0:1]).then_inc(tanh_done, 1)

            def g_high(b, m):
                act.wait_ge(post_used, NPOST * b + POST_USED["B", m] + 1)
                act.copy(gT[:, 0, m, :], g[:, m % 2, :]).then_inc(ghi_done, 1)

            def iteration(i, att, pre, post):
                for t in range(8 * QUADS):
                    k, m = t // 8, t % 8
                    if m == 3 and (att if k < 7 else pre):
                        copy_max_rows(*job_batch("att", "MT", k, i))
                    if m == 7 and (att if k else post):
                        copy_o(*((i, k - 1) if k else (i - 1, QUADS - 1)))
                    if att and k == 0 and m - 1 in PV_SLOTS:
                        move_v(i, PV_SLOTS.index(m - 1))
                    for cat, name, n in JOBS.get(t - 1, ()):
                        if not runs(cat, name, n, att, pre, post):
                            continue
                        if name == "X1T":
                            copy_x1T(i + 1, n)
                        elif name == "QK":
                            copy_raw(i + 1, n)
                        elif name == "V":
                            copy_v(i + 1, n)
                        elif name == "AT":
                            copy_attnT(i - 1, n)
                        elif name == "X2T":
                            x2_high(i - 1, n)
                        elif name == "A":
                            tanh(i - 1, n)
                    if att:
                        exps(i, k, m)
                    if pre:
                        for n in CAST_AT.get(t, ()):
                            cast_part(i + 1, n)
                    for cat, name, n in JOBS.get(t - 1, ()):
                        if name == "B" and post:
                            g_high(i - 1, n)
                if pre:
                    copy_v(i + 1, 1)

            act.wait_ge(lam_sum, 3)
            act.activation(lam_e[:, :], lam_s[:, :], ACT.Exp).then_inc(lam_exp, 1)
            for c in range(EC):
                copy_x1T(0, c)
            for j in range(4):
                copy_raw(0, j)
            act.wait_ge(consts, 5)
            for h in range(2):
                copy_v(0, h)
            for n in range(CASTS):
                cast_part(0, n)
            copy_max_rows(0, 0)
            act.wait_ge(ternary, 3)
            iteration(0, True, True, False)
            with act.Fori(*LOOP) as i:
                iteration(i, True, True, True)
            iteration(B - 1, True, False, True)
            iteration(B, False, False, True)

        @block.vector
        def _(dve):
            def row_maxima(b, q, m):
                for j in range(2):
                    dve.wait_ge(s_ready, 128 * b + 16 * q + 2 * m + j + 1)
                    dve.tensor_reduce(row_max[:, q % 2, m // 2, m % 2, j:j + 1], s_bank[S_BANKS[2 * m + j]][:, :], AX.X,
                                      ALU.max).then_inc(s_used, 1)

            def split_max_high(b, q):
                dve.wait_ge(s_used, 128 * b + 16 * q + 16)
                wait(dve, mt_ready, 8 * b + q)
                dve.tensor_scalar(max_parts[:, :, :, :, 0], row_max[:, q % 2], -1.0, None,
                                  ALU.mult).then_inc(max_hi, 1)

            def split_max_low(b, q):
                dve.wait_ge(max_hi, 8 * b + q + 1)
                dve.scalar_tensor_tensor(out=max_parts[:, :, :, :, 1], in0=row_max[:, q % 2], scalar=-1.0,
                                         in1=max_parts[:, :, :, :, 0], op0=ALU.mult,
                                         op1=ALU.subtract).then_inc(max_split, 1)

            def o_view(q):
                return d_bank[BANK["OT", (q + 2) % 8]][:, :].rearrange("p (n s e) -> p n s e", n=NT, s=4)

            def out_recip(b, q):
                dve.wait_ge(ot_ready, 8 * b + q + 1)
                dve.reciprocal(o_recip[:, :, :], o_view(q)[:, :, :, VD]).then_inc(o_step, 1)

            def out_scale_heads(b, q):
                dve.wait_ge(o_step, 48 * b + 6 * q + 1)
                dve.tensor_tensor(o_scaled[:, :, :, :], o_view(q)[:, :, :, 0:VD],
                                  o_recip[:, :, :].unsqueeze(3).to_broadcast([P, NT, 4, VD]), ALU.mult).then_inc(ot_used, 1)

            def out_diff(b, q):
                dve.wait_ge(ot_used, 8 * b + q + 1)
                if q == 0 and isinstance(b, int) and b == 0:
                    dve.wait_ge(lam_done, 2)
                v = o_scaled[:, :, :, :].rearrange("p n (a j) e -> p n a j e", j=2)
                dve.scalar_tensor_tensor(out=o_diff[:, :, :, :], in0=v[:, :, :, 1], scalar=neg_lam[:, 0:1],
                                         in1=v[:, :, :, 0], op0=ALU.mult, op1=ALU.add).then_inc(o_step, 1)

            def out_clamp(b, q):
                dve.wait_ge(o_step, 48 * b + 6 * q + 2)
                dve.tensor_scalar(o_sq[:, :, :, :], o_diff[:, :, :, :], SQUARE_MAX, -SQUARE_MAX, ALU.min,
                                  ALU.max).then_inc(o_step, 1)

            def out_square(b, q):
                dve.wait_ge(o_step, 48 * b + 6 * q + 3)
                dve.scalar_tensor_tensor(out=o_sq[:, :, :, :], in0=o_sq[:, :, :, :], scalar=1.0 / VD,
                                         in1=o_sq[:, :, :, :], op0=ALU.mult, op1=ALU.mult).then_inc(o_step, 1)

            def out_sum(b, q):
                dve.wait_ge(o_step, 48 * b + 6 * q + 4)
                dve.tensor_reduce(o_ss[:, :], o_sq[:, :, :, :].rearrange("p n a e -> p (n a) e"), AX.X,
                                  ALU.add).then_inc(o_step, 1)

            def out_eps(b, q):
                dve.wait_ge(o_step, 48 * b + 6 * q + 5)
                dve.tensor_scalar(o_ms[:, :], o_ss[:, :], EPS, None, ALU.add).then_inc(o_step, 1)

            def out_mask(b, q):
                dve.wait_ge(o_rms_done, 8 * b + q + 1)
                dve.scalar_tensor_tensor(out=o_rms_in[:, :], in0=o_ms[:, :], scalar=MEAN_MAX, in1=o_rms[:, :],
                                         op0=ALU.is_lt, op1=ALU.mult).then_inc(o_masked, 1)

            def out_norm(b, q):
                dve.wait_ge(o_masked, 8 * b + q + 1)
                if q == 0:
                    wait(dve, post_ready, NPOST * (b - 1) + POST_USED["AT", 1] + 1)
                dve.tensor_tensor(attn[:, :, q * 2 * VD:(q + 1) * 2 * VD].rearrange("p n (a e) -> p n a e", a=2),
                                  o_diff[:, :, :, :],
                                  o_rms_in[:, :].rearrange("p (n a) -> p n a", a=2).unsqueeze(3).to_broadcast([P, NT, 2, VD]),
                                  ALU.mult).then_inc(o_norm, 1)

            def ln_stats(s, src, b, tiles=range(NT)):
                for n in tiles:
                    dve.bn_stats(stats[s][:, n, :], src[:, n, :]).then_inc(ln_step[s], 1)

            def ln_stats_written(s, b):
                dve.wait_ge(ln_step[s], 9 * b + 4)

            def ln_aggregate(s, b):
                for n in range(NT):
                    dve.bn_aggr(mean_var[s][:, n, :], stats[s][:, n, :]).then_inc(ln_step[s], 1)

            def ln_variance(s, b):
                dve.wait_ge(ln_step[s], 9 * b + 8)
                dve.tensor_scalar(var_eps[s][:, :], mean_var[s][:, :, 1], EPS, None, ALU.add).then_inc(ln_step[s], 1)

            def ln_apply(s, src, dst, b, tiles=range(NT)):
                if tiles[0] == 0:
                    dve.wait_ge(ln_rstd[s], b + 1)
                if s == 0 and tiles[0] == 0:
                    wait(dve, pre_ready, NPRE * (b - 1) + 2)
                    wait(dve, glo_done, NB * (b - 2))
                for n in tiles:
                    dve.tensor_scalar(dst[:, n, :], src[:, n, :], mean_var[s][:, n, 0:1], rstd[s][:, n:n + 1],
                                      ALU.subtract, ALU.mult).then_inc(ln_out[s], 1)

            def residual(b, h):
                dve.wait_ge(post_ready, NPOST * b + POST_USED["OP", h] + 1)
                if h == 0:
                    dve.wait_ge(ld_xres, 16 * b + 16)
                    wait(dve, out_stored, 16 * b)
                dve.tensor_tensor(x2[:, 2 * h:2 * h + 2, :],
                                  d_bank[BANK["OP", h]][:, :].rearrange("p (n e) -> p n e", n=2),
                                  x_res[:, 2 * h:2 * h + 2, :], ALU.add).then_inc(post_used, 1)

            def x2_low(b, c):
                dve.wait_ge(x2h_done, 2 * b + c + 1)
                dve.tensor_tensor(x2T[:, 1, c, :], d_bank[BANK["X2T", c]][:, :], x2T[:, 0, c, :],
                                  ALU.subtract).then_inc(post_used, 1)

            def gate_a(b, m):
                dve.wait_ge(post_used, NPOST * b + POST_USED["A", m])
                dve.wait_ge(tanh_done, NB * b + m + 1)
                dve.scalar_tensor_tensor(out=gate[:, :], in0=th[:, m % 2, :], scalar=1.0,
                                         in1=d_bank[BANK["A", m]][0:HB, :], op0=ALU.add,
                                         op1=ALU.mult).then_inc(post_used, 1)

            def gate_b(b, m):
                dve.wait_ge(post_used, NPOST * b + POST_USED["A", m] + 1)
                dve.wait_ge(post_ready, NPOST * b + POST_USED["B", m] + 1)
                wait(dve, glo_done, NB * b + max(m - 1, 0))
                dve.scalar_tensor_tensor(out=g[:, m % 2, :], in0=gate[:, :], scalar=0.125,
                                         in1=d_bank[BANK["B", m]][0:HB, :], op0=ALU.mult,
                                         op1=ALU.mult).then_inc(post_used, 1)

            def finish(b, h):
                dve.wait_ge(post_ready, NPOST * b + POST_USED["DN", h] + 1)
                dve.scalar_tensor_tensor(out=x2[:, 2 * h:2 * h + 2, :],
                                         in0=d_bank[BANK["DN", h]][:, :].rearrange("p (n e) -> p n e", n=2),
                                         scalar=out_scale[:, 0:1], in1=x2[:, 2 * h:2 * h + 2, :], op0=ALU.mult,
                                         op1=ALU.add).then_inc(post_used, 1)

            def iteration(i, att, pre, post):
                for t in range(8 * QUADS):
                    k, m = t // 8, t % 8
                    if att if k < 7 else pre:
                        b, q = job_batch("att", "MT", k, i)
                        if m == 0:
                            split_max_high(b, q)
                        if m == 1:
                            split_max_low(b, q)
                    if m in (1, 2) and (att if k >= 3 else post):
                        (out_mask, out_norm)[m - 1](*((i, k - 3) if k >= 3 else (i - 1, k + 5)))
                    if att if k >= 2 else post:
                        b, q = job_batch("att", "OT", k, i)
                        for at, step in ((2, out_recip), (2, out_scale_heads), (4, out_diff), (5, out_clamp),
                                         (6, out_square), (6, out_sum), (7, out_eps)):
                            if m == at:
                                step(b, q)
                    if pre:
                        if t == LN1_AT[0]:
                            dve.wait_ge(ld_x, 16 * (i + 1) + 16)
                        if LN1_AT[0] <= t < LN1_AT[0] + 2:
                            ln_stats(0, x_pre, i + 1, [2 * (t - LN1_AT[0]), 2 * (t - LN1_AT[0]) + 1])
                        if t == LN1_AT[1]:
                            ln_aggregate(0, i + 1)
                        if t == LN1_AT[2]:
                            ln_variance(0, i + 1)
                        if LN1_AT[3] <= t < LN1_AT[3] + 2:
                            ln_apply(0, x_pre, x1n, i + 1, [2 * (t - LN1_AT[3]), 2 * (t - LN1_AT[3]) + 1])
                    if post:
                        for h in range(2):
                            if t == OP_AT[h] + 1:
                                residual(i - 1, h)
                            if t == OP_AT[h] + 2:
                                dve.wait_ge(post_used, NPOST * (i - 1) + POST_USED["OP", h] + 1)
                                ln_stats(1, x2, i - 1, [2 * h, 2 * h + 1])
                        if t == LN2_AT[1]:
                            ln_aggregate(1, i - 1)
                        if t == LN2_AT[2]:
                            ln_variance(1, i - 1)
                        if LN2_AT[3] <= t < LN2_AT[3] + 2:
                            ln_apply(1, x2, x2n, i - 1, [2 * (t - LN2_AT[3]), 2 * (t - LN2_AT[3]) + 1])
                        for cat, name, n in JOBS.get(t - 2, ()):
                            if name == "X2T":
                                x2_low(i - 1, n)
                            if name == "A":
                                gate_a(i - 1, n)
                        for cat, name, n in JOBS.get(t - 1, ()):
                            if name == "B":
                                gate_b(i - 1, n)
                            if name == "DN":
                                finish(i - 1, n)
                    if t == LN1_AT[1] - 1 and pre:
                        ln_stats_written(0, i + 1)
                    if t == LN2_AT[1] - 1 and post:
                        ln_stats_written(1, i - 1)
                    if k + 2 < QUADS and att:
                        row_maxima(i, k + 2, m)
                    if k + 2 >= QUADS and pre:
                        row_maxima(i + 1, k + 2 - QUADS, m)

            dve.memset(ones[:, :], 1.0).then_inc(consts, 1)
            dve.memset(minus_half[:, :], -0.5).then_inc(consts, 1)
            dve.memset(v_next[:, :, :, VD:VD + 1], 1.0).then_inc(consts, 1)
            dve.memset(o_bank[:, :], 0.0).then_inc(consts, 1)
            dve.memset(abs_sums[:, :], 0.0).then_inc(abs_done, 1)
            dve.wait_ge(ld_w["ident"], 16)
            dve.tensor_copy(identb[:, :], ident[:, :]).then_inc(consts, 1)
            dve.wait_ge(ld_x, 16)
            ln_stats(0, x_pre, 0)
            ln_stats_written(0, 0)
            ln_aggregate(0, 0)
            ln_variance(0, 0)
            dve.wait_ge(ld_w["small"], 32)
            dve.tensor_tensor(lam_p[:, 0], lam_v[:, 0], lam_v[:, 1], ALU.mult).then_inc(lam_sum, 1)
            ln_apply(0, x_pre, x1n, 0)
            dve.tensor_tensor(lam_p[:, 1], lam_v[:, 2], lam_v[:, 3], ALU.mult).then_inc(lam_sum, 1)
            dve.wait_ge(lam_sum, 2)
            dve.tensor_reduce(lam_s[:, :], lam_p[:, :, :], AX.X, ALU.add).then_inc(lam_sum, 1)
            dve.wait_ge(abs_done, 1)
            dve.wait_ge(ld_w["tern"], 48)
            for w in range(2):
                dve.tensor_reduce(abs_sums[:, w:w + 1], w13_raw[:, w].rearrange("p c h -> p (c h)"), AX.X, ALU.add,
                                  apply_absolute_value=True).then_inc(abs_done, 1)
            dve.tensor_reduce(abs_sums[0:HB, 2:3], w2_raw.rearrange("p m e -> p (m e)"), AX.X, ALU.add,
                              apply_absolute_value=True).then_inc(abs_done, 1)
            dve.wait_ge(ld_w["vo"], 32)
            for c in range(EC):
                dve.tensor_scalar(wo_sb[:, c, :], wo_sb[:, c, :], gcol[:, 0:1], 1.0 - LAMBDA_INIT, ALU.mult,
                                  ALU.mult).then_inc(wo_scaled, 1)
            dve.wait_ge(lam_exp, 1)
            dve.tensor_scalar(neg_lam[:, :], lam_e[:, 1:2], -LAMBDA_INIT, None, ALU.add).then_inc(lam_done, 1)
            dve.wait_ge(lam_done, 1)
            dve.tensor_tensor(neg_lam[:, :], neg_lam[:, :], lam_e[:, 0:1], ALU.subtract).then_inc(lam_done, 1)
            dve.wait_ge(scale_ready, 1)
            dve.tensor_scalar(scales[:, :], d_bank[0][:, 0:3], 1.0 / (HIDDEN * E), None, ALU.mult).then_inc(setup, 1)
            dve.wait_ge(setup, 1)
            dve.tensor_scalar(half[:, :], scales[:, :], 0.5, None, ALU.mult).then_inc(setup, 1)
            dve.tensor_scalar(neg_half[:, :], scales[:, :], -0.5, None, ALU.mult).then_inc(setup, 1)
            dve.tensor_tensor(s13[:, :], scales[:, 0:1], scales[:, 1:2], ALU.mult).then_inc(setup, 1)
            dve.wait_ge(setup, 4)
            dve.scalar_tensor_tensor(out=out_scale[:, :], in0=s13[:, :], scalar=4.0, in1=scales[:, 2:3],
                                     op0=ALU.mult, op1=ALU.mult).then_inc(setup, 1)
            for w, (rawv, dst) in enumerate(((w13_raw[:, 0].rearrange("p c h -> p (c h)"), t13[:, 0].rearrange("p c h -> p (c h)")),
                                             (w13_raw[:, 1].rearrange("p c h -> p (c h)"), t13[:, 1].rearrange("p c h -> p (c h)")),
                                             (w2_raw.rearrange("p m e -> p (m e)"), t2[:, :, :].rearrange("p m e -> p (m e)")))):
                rows, n = rawv.shape
                wait(dve, ternary, w)
                dve.tensor_scalar(below[0:rows, 0:n], rawv, neg_half[0:rows, w:w + 1], None, ALU.is_lt).then_inc(setup, 1)
                dve.wait_ge(setup, 6 + w)
                dve.scalar_tensor_tensor(out=dst, in0=rawv, scalar=half[0:rows, w:w + 1], in1=below[0:rows, 0:n],
                                         op0=ALU.is_gt, op1=ALU.subtract).then_inc(ternary, 1)
            for m in range(SLOTS):
                row_maxima(0, 0, m)
            split_max_high(0, 0)
            split_max_low(0, 0)
            for m in range(SLOTS):
                row_maxima(0, 1, m)
            iteration(0, True, True, False)
            with dve.Fori(*LOOP) as i:
                iteration(i, True, True, True)
            iteration(B - 1, True, False, True)
            iteration(B, False, False, True)

        @block.gpsimd
        def _(pool):
            def rope_ops(b, first, last):
                for n in range(first, last):
                    wait(pool, rope_step, ROPE * b + n)
                    rotate_and_split(b, n)

            def rotate_and_split(b, n):
                cos, sin = cos_sin[:, 0, :], cos_sin[:, 1, :]
                for side, base in ((0, 0), (1, 8)):
                    even, odd, rot = raw[:, 2 * side, :], raw[:, 2 * side + 1, :], roped_even[:, side, :]
                    if n == base:
                        pool.wait_ge(pre_used, NPRE * b + PRE_USED["QK", 2 * side + 1] + 1)
                        return pool.tensor_tensor(rot, even, cos, ALU.mult).then_inc(rope_step, 1)
                    if n == base + 1:
                        return pool.tensor_tensor(rope_tmp[:, :], odd, sin, ALU.mult).then_inc(rope_step, 1)
                    if n == base + 2:
                        return pool.tensor_tensor(rot, rot, rope_tmp[:, :], ALU.subtract).then_inc(rope_step, 1)
                    if n == base + 3:
                        return pool.tensor_tensor(even, even, sin, ALU.mult).then_inc(rope_step, 1)
                    if n == base + 4:
                        return pool.tensor_tensor(odd, odd, cos, ALU.mult).then_inc(rope_step, 1)
                    if n == base + 5:
                        return pool.tensor_tensor(odd, even, odd, ALU.add).then_inc(rope_step, 1)
                side = 0 if n in (6, 7, 14, 15) else 1
                part = 0 if n in (6, 7, 16, 17) else 1
                a = n % 2
                v = roped_even[:, side, :] if a == 0 else raw[:, 2 * side + 1, :]
                pool.wait_ge(cast_done, CASTS * b + 4 * side + 2 * part + a + 1)
                dst = v if part == 0 else parts[:, side, 2, a, :]
                pool.tensor_tensor(dst, v, parts[:, side, part, a, :], ALU.subtract).then_inc(rope_step, 1)

            def ln_power(s, b):
                pool.wait_ge(ln_step[s], 9 * b + 9)
                pool.tensor_tensor(rstd[s][:, :], var_eps[s][:, :], minus_half[:, 0:NT], ALU.pow).then_inc(ln_rstd[s], 1)

            def out_power(b, q):
                pool.wait_ge(o_step, 48 * b + 6 * q + 6)
                wait(pool, o_masked, 8 * b + q)
                pool.tensor_tensor(o_rms[:, :], o_ms[:, :], minus_half[:, :], ALU.pow).then_inc(o_rms_done, 1)

            def g_low(b, m):
                pool.wait_ge(ghi_done, NB * b + m + 1)
                pool.tensor_tensor(gT[:, 1, m, :], g[:, m % 2, :], gT[:, 0, m, :], ALU.subtract).then_inc(glo_done, 1)

            def iteration(i, att, pre, post):
                for t in range(8 * QUADS):
                    k = t // 8
                    if pre and t == LN1_AT[2]:
                        ln_power(0, i + 1)
                    if pre and t in ROPE_AT:
                        rope_ops(i + 1, *ROPE_AT[t])
                    if post and t == LN2_AT[2]:
                        ln_power(1, i - 1)
                    for cat, name, n in JOBS.get(t - 2, ()):
                        if name == "B" and post:
                            g_low(i - 1, n)
                    if t % 8 == 7 and (att if k >= 2 else post):
                        out_power(*job_batch("att", "OT", k, i))

            pool.wait_ge(consts, 5)
            ln_power(0, 0)
            pool.wait_ge(ld_w["rope"], 16)
            rope_ops(0, 0, 20)
            iteration(0, True, True, False)
            with pool.Fori(*LOOP) as i:
                iteration(i, True, True, True)
            iteration(B - 1, True, False, True)
            iteration(B, False, False, True)


def rope_tables():
    angle = (1.0 / np.float32(1250) ** np.linspace(0.0, 1.0, HD // 2, dtype=np.float32)).astype(np.float32)
    freqs = np.arange(T, dtype=np.float32)[:, None] * angle
    rows = np.tile(freqs.T, (2 * H, 1)).astype(np.float32)
    return np.stack([np.cos(rows), np.sin(rows)]).astype(np.float32)


def kernel(**inputs):
    import ml_dtypes
    import concourse.bacc as bacc
    from concourse.bass_utils import run_bass_kernel_spmd

    a = {k: np.asarray(v) for k, v in inputs.items()}

    def rotary_pairs(w):
        return w.reshape(2 * H, HD // 2, 2, E).transpose(3, 2, 0, 1).reshape(E, 2, P)

    def pad_hidden(w):
        return np.concatenate([w, np.zeros((HPAD - HIDDEN,) + w.shape[1:], w.dtype)])

    pads = np.zeros((2, HD // 2, BLOCK - SHIFT_ROW, T), ml_dtypes.bfloat16)
    pads[1, 0, 0:2] = 1
    pads = pads.reshape(2, HD // 2, -1)
    arrays = {
        "x": a["L0_attn_x"],
        "wqk": np.concatenate([rotary_pairs(a["L0_attn_Wq"]), rotary_pairs(a["L0_attn_Wk"])], axis=1),
        "wv": a["L0_attn_Wv"].T, "wo": a["L0_attn_Wo"].T,
        "w1": pad_hidden(a["L0_ffn_w1"]).T, "w3": pad_hidden(a["L0_ffn_w3"]).T, "w2": pad_hidden(a["L0_ffn_w2"].T),
        "rope": rope_tables(), "ident": np.eye(P, dtype=np.float32), "pads": pads,
        "lam": np.stack([a["L0_attn_lambda_q1"], a["L0_attn_lambda_k1"], a["L0_attn_lambda_q2"], a["L0_attn_lambda_k2"]]),
        "gamma": np.tile(a["L0_attn_gamma"], P // VD).reshape(P, 1),
    }
    arrays = {f"in_{k}": np.ascontiguousarray(v) for k, v in arrays.items()}
    nc = bacc.Bacc("TRN2", target_bir_lowering=False, num_devices=1)
    args = [nc.dram_tensor(k, v.shape, mybir.dt.from_np(v.dtype), kind="ExternalInput").ap() for k, v in arrays.items()]
    out = nc.dram_tensor("out", (B, T, E), F32, kind="ExternalOutput").ap()
    build(nc, *args, out)
    r = run_bass_kernel_spmd(nc, [arrays], core_ids=[0])
    return r.results[0]["out"]
```

```python
from contextlib import ExitStack

import numpy as np

import concourse.bass as bass
from concourse import mybir

F32, BF16, F16 = mybir.dt.float32, mybir.dt.bfloat16, mybir.dt.float16
ALU = mybir.AluOpType
ACT = mybir.ActivationFunctionType
AX = mybir.AxisListType

B, T, E = 8, 512, 256
H, HD = 16, 8
VD = 2 * HD
P = 128
NT = T // P
EC = E // P
HIDDEN = int(2 * E * 4 / 3)
HB = 114
NB = -(-HIDDEN // HB)
HPAD = HB * NB
QUADS = 2 * H // 4
SLOTS = 8
ROWS = 64
BLOCK = ROWS // (HD // 2)
SHIFT_ROW = 12
LAMBDA_INIT = 0.8 - 0.6 * float(np.exp(-0.3 * 12))
EPS = 1e-5
SQUARE_MAX = 2.0 ** 64 * (1 - 2.0 ** -20)
MEAN_MAX = 2.0 ** 124 * (1 - 2.0 ** -18)
SCALE = HD ** -0.5
HALF_SUM = 2.0 ** 15
FLOOR = 1e-30
PASSES = ((0, 0), (0, 1), (1, 0))
Q_BLOCKS = ((0, 1, 3), (3, 2, 2), (4, 1, 1))
K_BLOCKS = ((2, 1, 3), (0, 5, 2), (1, 1, 1))
PV_SLOTS = (0, 2, 4, 6)
TILES = 16 * QUADS
S_BANKS = [n % 3 for n in range(TILES - 1)] + [1]

JOBS = {}


def _place(t, *job):
    JOBS.setdefault(t, []).append(job)


X1T_LAG = 1
AT_LAG = 2
X1T_AT = (7, 8)
QK_AT = (9, 11, 13, 15)
AT_AT = (18, 19)
OP_AT = (21, 23)
X2T_AT = (31, 33)
A_AT = (35, 39, 43, 47, 53, 59)
B_AT = (37, 41, 45, 51, 55, 61)
DN_AT = (3, 4, 5, 6)
V_AT = (29, 62)
LN1_AT = (1, 3, 4, 5)
LN2_AT = (23, 27, 28, 30)
ROPE_AT = {13: (0, 6), 18: (6, 11), 20: (11, 14), 24: (14, 18), 30: (18, 20)}
CAST_AT = {18: (0, 1), 21: (2, 3), 24: (4, 5), 28: (6, 7)}
for _c in range(EC):
    _place(X1T_AT[_c], "pre", "X1T", _c)
for _j, _t in enumerate(QK_AT):
    _place(_t, "pre", "QK", _j)
for _h in range(2):
    _place(V_AT[_h], "pre", "V", _h)
for _k in range(QUADS):
    _place(8 * _k + 1, "att", "OT", _k)
    _place(8 * _k + 2, "att", "MT", _k)
for _n in range(2):
    _place(AT_AT[_n], "post", "AT", _n)
    _place(OP_AT[_n], "post", "OP", _n)
    _place(X2T_AT[_n], "post", "X2T", _n)
for _m in range(NB):
    _place(A_AT[_m], "post", "A", _m)
    _place(B_AT[_m], "post", "B", _m)
for _n in range(NT):
    _place(DN_AT[_n], "down", "DN", _n)
LAST_JOBS = {}
for _t, _jobs in JOBS.items():
    for _cat, _name, _n in _jobs:
        _t2 = {"A": 35 + 2 * _n, "B": 37 + 2 * _n, "DN": 14 + _n}.get(_name, _t)
        LAST_JOBS.setdefault(_t2, []).append((_cat, _name, _n))


def jobs_at(t, i):
    return (LAST_JOBS if isinstance(i, int) and i == B else JOBS).get(t, ())


ORDER = [job for t in sorted(JOBS) for job in JOBS[t]]
BANK = {job[1:]: n % 2 for n, job in enumerate(ORDER)}
PRE_USED = {("X1T", c): c for c in range(EC)} | {("QK", j): 2 + j for j in range(4)} | {("V", h): 6 + h for h in range(2)}
POST_USED = ({("AT", n): n for n in range(2)} | {("OP", n): 2 + n for n in range(2)} | {("X2T", n): 4 + n for n in range(2)}
             | {("A", m): 6 + 2 * m for m in range(NB)} | {("B", m): 7 + 2 * m for m in range(NB)})
NPRE, NPOST = len(PRE_USED), len(POST_USED)


def job_batch(cat, name, k, i):
    if cat == "pre":
        return i + 1, k
    if cat == "post":
        return i - 1, k
    if cat == "down":
        return i - 2, k
    if name == "OT":
        return (i, k - 2) if k >= 2 else (i - 1, k + 6)
    return (i, k + 1) if k < 7 else (i + 1, 0)


def wait(eng, sem, value):
    if not isinstance(value, int) or value > 0:
        eng.wait_ge(sem, value)


def build(nc, x, wqk, wv, wo, w1, w3, w2, rope, ident_in, pads, lam_in, gamma_in, out):
    with ExitStack() as ctx:
        def sb(name, shape, dt):
            return ctx.enter_context(nc.sbuf_tensor(name, shape, dt))

        def pb(name, shape, dt):
            return ctx.enter_context(nc.psum_tensor(name, shape, dt))

        def sem(name):
            return ctx.enter_context(nc.semaphore(name))

        scratch = [nc.dram_tensor(f"stack_{s}", [2 * H, ROWS, T], BF16).ap() for s in "qk"]

        ident = sb("ident", [P, P], F32)
        identb = sb("identb", [P, P], BF16)
        ones = sb("ones", [P, P], F32)
        minus_half = sb("minus_half", [P, 8], F32)
        wqk_parts = sb("wqk_parts", [P, 2, EC, 4, P], F16)
        wv_parts = sb("wv_parts", [P, 2, EC, E], F16)
        wo_parts = sb("wo_parts", [P, 2, EC, E], F16)
        unscale = sb("unscale", [P, 3], F32)
        upscale = sb("upscale", [P, 3], F32)
        t13 = sb("t13", [P, 2, EC, HPAD], F16)
        t2 = sb("t2", [HB, NB, E], F16)
        cos_sin = sb("cos_sin", [P, 2, T], F32)
        gcol = sb("gcol", [P, 1], F32)
        lam_v = sb("lam_v", [P, 4, HD], F32)
        lam_p = sb("lam_p", [P, 2, HD], F32)
        lam_s = sb("lam_s", [P, 2], F32)
        lam_e = sb("lam_e", [P, 2], F32)
        neg_lam = sb("neg_lam", [P, 1], F32)
        abs_sums = sb("abs_sums", [P, 6], F32)
        scales = sb("scales", [P, 3], F32)
        half = sb("half", [P, 3], F32)
        neg_half = sb("neg_half", [P, 3], F32)
        s13 = sb("s13", [P, 1], F32)
        out_scale = sb("out_scale", [P, 1], F32)
        q_stack = sb("q_stack", [P, QUADS, 2, T], BF16)
        k_stack = sb("k_stack", [P, QUADS, 2, T], BF16)
        probs = sb("probs", [P, 2, NT, 4, T], F32)
        v_next = sb("v_next", [P, NT, H, VD + 1], F32)
        v_sb = sb("v_sb", [P, NT, H, VD + 1], F32)
        x_pre = sb("x_pre", [P, NT, E], F32)
        x_res = sb("x_res", [P, NT, E], F32)
        x1n = sb("x1n", [P, NT, E], F32)
        g = x1n[0:HB].rearrange("p (a n) e -> p a (n e)", a=2)
        xhT = sb("xhT", [P, 2, EC, T], F16)
        raw = sb("raw", [P, 4, T], F32)
        roped_even = sb("roped_even", [P, 2, T], F32)
        rope_tmp = sb("rope_tmp", [P, T], F32)
        parts = sb("parts", [P, 2, 3, 2, T], BF16)
        row_max = sb("row_max", [P, 2, NT, 2, 2], F32)
        max_parts = sb("max_parts", [P, NT, 2, 2, 2], BF16)
        max_rows = sb("max_rows", [8, 2, T], BF16)
        o_sb = sb("o_sb", [P, T], F32)
        o_recip = sb("o_recip", [P, NT, 4], F32)
        o_scaled = sb("o_scaled", [P, NT, 4, VD], F32)
        o_diff = sb("o_diff", [P, NT, 2, VD], F32)
        o_sq = sb("o_sq", [P, NT, 2, VD], F32)
        o_ss = sb("o_ss", [P, 8], F32)
        o_ms = sb("o_ms", [P, 8], F32)
        o_rms = sb("o_rms", [P, 8], F32)
        o_rms_in = sb("o_rms_in", [P, 8], F32)
        attn = sb("attn", [P, NT, E], F32)
        attnT = sb("attnT", [P, EC, T], F32)
        attn_parts = attnT[:, :, :].rearrange("p c t -> p (c t)").bitcast(F16).rearrange("p (a c t) -> p a c t", a=2, c=EC)
        x2 = sb("x2", [P, NT, E], F32)
        x2n = attnT[:, :, :].rearrange("p c (n e) -> p (c n) e", e=E)
        stats = [sb(f"stats{n}", [P, NT, 6], F32) for n in (1, 2)]
        mean_var = [sb(f"mean_var{n}", [P, NT, 2], F32) for n in (1, 2)]
        var_eps = [sb(f"var_eps{n}", [P, NT], F32) for n in (1, 2)]
        rstd = [sb(f"rstd{n}", [P, NT], F32) for n in (1, 2)]
        x2T = sb("x2T", [P, 2, EC, T], F16)
        th = x_res[0:HB].rearrange("p (a n) e -> p a (n e)", a=2)
        gate = sb("gate", [HB, T], F32)
        gT = sb("gT", [HB, 2, NB, T], F16)

        late = probs[:, 1].rearrange("p c s t -> p (c s t)")
        w13_raw = late[:, 0:2 * EC * HPAD].rearrange("p (w c h) -> p w c h", w=2, c=EC)
        w2_raw = late[0:HB, 2 * EC * HPAD:2 * EC * HPAD + NB * E].rearrange("p (m e) -> p m e", m=NB)
        below = late[:, 2 * EC * HPAD + NB * E:2 * EC * HPAD + NB * E + NB * E]
        raw_at = 2 * EC * HPAD + 2 * NB * E
        wqk_raw = late[:, raw_at:raw_at + EC * 4 * P].rearrange("p (c j m) -> p c j m", c=EC, j=4)
        wv_raw = late[:, raw_at + EC * 4 * P:raw_at + EC * 4 * P + EC * E].rearrange("p (c e) -> p c e", c=EC)
        wo_raw = late[:, raw_at + EC * 4 * P + EC * E:raw_at + EC * 4 * P + 2 * EC * E].rearrange("p (c e) -> p c e", c=EC)

        st_bank = [pb(f"st{n}", [P, T], F32) for n in range(2)]
        s_bank = [pb(f"s{n}", [P, T], F32) for n in range(3)]
        o_bank = pb("o_bank", [P, T], F32)
        d_bank = [pb(f"d{n}", [P, T], F32) for n in range(2)]

        ld_x = sem("ld_x")
        ld_xres = sem("ld_xres")
        ld_w = {n: sem(f"ld_{n}") for n in ("ident", "qk", "rope", "vo", "tern", "small", "pads")}
        scr_written = sem("scr_written")
        stack_loaded = [sem(f"stack_loaded{q}") for q in range(QUADS)]
        shift_loaded = [sem(f"shift_loaded{n}") for n in range(2)]
        out_stored = sem("out_stored")
        consts = sem("consts")
        abs_done = sem("abs_done")
        scale_ready = sem("scale_ready")
        setup = sem("setup")
        lam_sum = sem("lam_sum")
        lam_exp = sem("lam_exp")
        lam_done = sem("lam_done")
        qk_summed = sem("qk_summed")
        qk_sum_ready = sem("qk_sum_ready")
        qk_unit = sem("qk_unit")
        qk_split = sem("qk_split")
        wo_scaled = sem("wo_scaled")
        vo_unit = sem("vo_unit")
        vo_split = sem("vo_split")
        xh_high = sem("xh_high")
        attn_high = sem("attn_high")
        ternary = sem("ternary")
        st_ready = sem("st_ready")
        s_ready = sem("s_ready")
        pv_done = sem("pv_done")
        pre_ready, mt_ready, ot_ready, post_ready, down_ready = (
            sem(n) for n in ("pre_ready", "mt_ready", "ot_ready", "post_ready", "down_ready"))
        pre_used, mt_used, ot_used, post_used, down_used = (
            sem(n) for n in ("pre_used", "mt_used", "ot_used", "post_used", "down_used"))
        exp_done = sem("exp_done")
        v_ready = sem("v_ready")
        o_copied = sem("o_copied")
        cast_done = sem("cast_done")
        x2h_done = sem("x2h_done")
        tanh_done = sem("tanh_done")
        ghi_done = sem("ghi_done")
        s_used = sem("s_used")
        max_hi = sem("max_hi")
        max_split = sem("max_split")
        o_step = sem("o_step")
        o_rms_done = sem("o_rms_done")
        o_masked = sem("o_masked")
        o_norm = sem("o_norm")
        ln_step = [sem(f"ln_step{n}") for n in (1, 2)]
        ln_rstd = [sem(f"ln_rstd{n}") for n in (1, 2)]
        ln_out = [sem(f"ln_out{n}") for n in (1, 2)]
        rope_step = sem("rope_step")
        first_rope = sem("first_rope")
        glo_done = sem("glo_done")

        QK_READY, LOOP = 2, (2, B - 1)
        CASTS, ROPE = 8, 20
        FIRST_CASTS = (0, 1, 4, 5, 2, 3, 6, 7)

        def rope_count(b, n):
            return ROPE * (b - 1) + 4 + n

        def job_used(name, n, b):
            if name == "OT":
                return ot_used, 8 * b + n + 1
            if name == "MT":
                return mt_used, 8 * b + n + 1
            if name == "DN":
                return down_used, NT * b + n + 1
            if (name, n) in PRE_USED:
                return pre_used, NPRE * b + PRE_USED[name, n] + 1
            return post_used, NPOST * b + POST_USED[name, n] + 1

        def runs(cat, name, k, att, pre, post, down):
            if cat == "pre":
                return pre
            if cat == "post":
                return post
            if cat == "down":
                return down
            if name == "OT":
                return att if k >= 2 else post
            return att if k < 7 else pre

        def job_bank(name, m, b):
            if isinstance(b, int) and b == B - 1:
                if name == "X2T":
                    return s_bank[1 + m]
                return (st_bank + s_bank)[(2 * m + "AB".index(name)) % 5]
            return d_bank[BANK[name, m]]

        x_v = x.rearrange("b (n p) e -> b p n e", p=P)
        out_v = out.rearrange("b (n p) e -> b p n e", p=P)
        block = ctx.enter_context(nc.Block())

        @block.sync
        def _(sp):
            def load_x(b, dst, done):
                sp.dma_start(dst[:, :, :], x_v[b]).then_inc(done, 16)

            def write_part(side, part):
                rows = scratch[side].rearrange("h (f c a) t -> (h f) c (a t)", c=BLOCK // 2, a=2)
                first, step, count = (Q_BLOCKS, K_BLOCKS)[side][part]
                src = parts[:, side, part].rearrange("p a t -> p (a t)")
                sp.dma_start(rows[:, first:first + step * (count - 1) + 1:step],
                             src.unsqueeze(1).to_broadcast([P, count, 2 * T])).then_inc(scr_written, 16)

            def write_parts(side, b):
                if side == 0:
                    for q in range(QUADS):
                        wait(sp, stack_loaded[q], 32 * b)
                sp.wait_ge(rope_step, rope_count(b, 16 if side == 0 else 20))
                for part in range(3):
                    write_part(side, part)

            def load_stack(b, q):
                if q == 0:
                    sp.wait_ge(scr_written, 96 * b + 96)
                if q == QUADS - 1:
                    wait(sp, st_ready, 128 * b)
                for side, dst in enumerate((q_stack, k_stack)):
                    src = scratch[side].rearrange("(g a j) r t -> g (j r) a t", a=2, j=2)
                    sp.dma_start(dst[:, q, :, :], src[q]).then_inc(stack_loaded[q], 16)

            def load_shift(b, q):
                sp.wait_ge(mt_used, 8 * b + q + 1)
                for pair in range(2):
                    for j in range(2):
                        r = 4 * pair + 2 * j
                        sp.dma_start(q_stack[64 * j + SHIFT_ROW:64 * j + SHIFT_ROW + 2, q, pair, :],
                                     max_rows[r:r + 2, q % 2, :]).then_inc(shift_loaded[q % 2], 16)

            def iteration(i, att, pre, post, down):
                if pre and not post:
                    sp.wait_ge(ln_out[0], 4)
                if pre:
                    load_x(i + 1, x_pre, ld_x)
                if att and post:
                    load_stack(i, 7)
                if post:
                    wait(sp, post_used, NPOST * (i - 1))
                    load_x(i - 1, x_res, ld_xres)
                for k in range(QUADS):
                    if down and k == 1:
                        sp.wait_ge(down_used, NT * (i - 1))
                        sp.dma_start(out_v[i - 2], x2[:, :, :]).then_inc(out_stored, 16)
                    if att and k < 7:
                        load_shift(i, k + 1)
                    if pre:
                        if k == 2:
                            write_parts(0, i + 1)
                        if k == 3:
                            write_parts(1, i + 1)
                        if k == 4:
                            for q in range(4):
                                load_stack(i + 1, q)
                        if k == 5:
                            load_stack(i + 1, 4)
                        if k == 6:
                            load_stack(i + 1, 5)
                        if k == 7:
                            load_shift(i + 1, 0)
                if pre:
                    load_stack(i + 1, 6)

            load_x(0, x_pre, ld_x)
            sp.dma_start(ident[:, :], ident_in).then_inc(ld_w["ident"], 16)
            sp.dma_start(wqk_raw, wqk.rearrange("(c p) j m -> p c j m", p=P)).then_inc(ld_w["qk"], 16)
            sp.dma_start(cos_sin[:, :, :], rope.rearrange("a p t -> p a t")).then_inc(ld_w["rope"], 16)
            sp.dma_start(lam_v[:, :, :], lam_in.partition_broadcast(P)).then_inc(ld_w["small"], 16)
            sp.dma_start(gcol[:, :], gamma_in).then_inc(ld_w["small"], 16)
            for w, src in enumerate((w1, w3)):
                sp.dma_start(w13_raw[:, w], src.rearrange("(c p) h -> p c h", p=P)).then_inc(ld_w["tern"], 16)
            sp.dma_start(w2_raw, w2.rearrange("(m p) e -> p m e", p=HB)).then_inc(ld_w["tern"], 16)
            sp.dma_start(wv_raw, wv.rearrange("(c p) e -> p c e", p=P)).then_inc(ld_w["vo"], 16)
            sp.dma_start(wo_raw, wo.rearrange("(c p) e -> p c e", p=P)).then_inc(ld_w["vo"], 16)
            for side in range(2):
                spare = scratch[side].rearrange("h (f r) t -> h f (r t)", r=BLOCK)[:, :, SHIFT_ROW * T:]
                sp.dma_start(spare, pads[side:side + 1].to_broadcast([2 * H, HD // 2, (BLOCK - SHIFT_ROW) * T])
                             ).then_inc(ld_w["pads"], 16)
            for done, value, side, part in ((cast_done, 2, 0, 0), (cast_done, 4, 1, 0), (cast_done, 6, 0, 1),
                                            (rope_step, 4, 0, 2), (cast_done, 8, 1, 1), (first_rope, 16, 1, 2)):
                sp.wait_ge(done, value)
                write_part(side, part)
            sp.wait_ge(ld_w["pads"], 32)
            for q in range(QUADS):
                load_stack(0, q)
            load_shift(0, 0)
            iteration(0, True, True, False, False)
            iteration(1, True, True, True, False)
            with sp.Fori(*LOOP) as i:
                iteration(i, True, True, True, True)
            iteration(B - 1, True, False, True, True)
            iteration(B, False, False, True, True)
            iteration(B + 1, False, False, False, True)
            sp.wait_ge(out_stored, 16 * B)

        @block.tensor
        def _(pe):
            last_on_bank = {}

            def take_bank(name, n, b):
                if name in ("X2T", "A", "B") and isinstance(b, int) and b == B - 1:
                    if (name, n) == ("X2T", 0):
                        pe.wait_ge(exp_done, 128 * B)
                        pe.wait_ge(s_used, 128 * B)
                    job = 2 * n + "AB".index(name) if name in "AB" else 0
                    if job >= 5:
                        pe.wait_ge(post_used, NPOST * b + POST_USED["AB"[(job - 5) % 2], (job - 5) // 2] + 1)
                    return job_bank(name, n, b)
                bank = BANK[name, n if name not in ("OT", "MT") else job_slot[name, n]]
                if bank in last_on_bank:
                    s, v = job_used(*last_on_bank[bank])
                    wait(pe, s, v)
                last_on_bank[bank] = (name, n, b)
                return d_bank[bank]

            def take_over(i):
                for cat, name, k in ORDER[-2:]:
                    b, q = job_batch(cat, name, k, i - 1)
                    last_on_bank[BANK[name, k]] = (name, q, b)

            job_slot = {("OT", q): (q + 2) % 8 for q in range(8)} | {("MT", q): (q - 1) % 8 for q in range(8)}

            def transposed_scores(b, q, m):
                if m == 0:
                    sem_q = shift_loaded[q % 2]
                    pe.wait_ge(sem_q, 256 * b + 64 * (q // 2) + 64)
                chunk, pair = m // 2, m % 2
                for j in range(2):
                    wait(pe, exp_done, 128 * b + 16 * q + 2 * m + j - 1)
                    rows = slice(64 * j, 64 * j + ROWS)
                    pe.matmul(st_bank[j][:, :], k_stack[rows, q, pair, chunk * P:chunk * P + P],
                              q_stack[rows, q, pair, :], start=True, stop=True).then_inc(st_ready, 1)

            def scores(b, q, m):
                if m == 0:
                    pe.wait_ge(stack_loaded[q], 32 * b + 32)
                tile, pair = m // 2, m % 2
                for j in range(2):
                    n = 16 * q + 2 * m + j
                    back = next(d for d in range(1, 7) if S_BANKS[(n - d) % TILES] == S_BANKS[n])
                    wait(pe, s_used, 128 * b + n - back + 1)
                    rows = slice(64 * j, 64 * j + ROWS)
                    pe.matmul(s_bank[S_BANKS[n]][:, :], q_stack[rows, q, pair, tile * P:tile * P + P],
                              k_stack[rows, q, pair, :], start=True, stop=True).then_inc(s_ready, 1)

            def values(b, q, c):
                pe.wait_ge(exp_done, 128 * b + 16 * q + 4 * c + 4)
                if q == 0:
                    pe.wait_ge(v_ready, 4 * b + c + 1)
                if c == 0:
                    wait(pe, o_copied, 8 * b + q)
                for slot in range(4):
                    head = 2 * q + slot // 2
                    mm = pe.matmul(o_bank[32 * slot:32 * slot + VD + 1, :], v_sb[:, c, head, :],
                                   probs[:, q % 2, c, slot, :], start=(c == 0), stop=(c == NT - 1))
                mm.then_inc(pv_done, 1)

            def transpose_tiles(d, src, idn):
                for n in range(NT):
                    t = pe.transpose(d[:, n * P:n * P + P], src(n), idn)
                return t

            def dense(name, n, b):
                d = take_bank(name, n, b)
                if name == "X1T":
                    pe.wait_ge(ln_out[0], 4 * b + 4)
                    transpose_tiles(d, lambda t: x1n[:, t, n * P:n * P + P], ident[:, :]).then_inc(pre_ready, 1)
                elif name == "QK":
                    pe.wait_ge(pre_used, NPRE * b + QK_READY)
                    for c in range(EC):
                        for w, a in PASSES:
                            mm = pe.matmul(d[:, :], wqk_parts[:, w, c, n, :], xhT[:, a, c, :],
                                           start=(c == 0 and (w, a) == PASSES[0]), stop=(c == EC - 1 and (w, a) == PASSES[-1]))
                    mm.then_inc(pre_ready, 1)
                elif name == "V":
                    for t in range(2 * n, 2 * n + 2):
                        for c in range(EC):
                            for w, a in PASSES:
                                mm = pe.matmul(d[:, (t % 2) * E:(t % 2) * E + E], xhT[:, a, c, t * P:t * P + P],
                                               wv_parts[:, w, c, :], start=(c == 0 and (w, a) == PASSES[0]),
                                               stop=(c == EC - 1 and (w, a) == PASSES[-1]))
                    mm.then_inc(pre_ready, 1)
                elif name == "MT":
                    pe.wait_ge(max_split, 8 * b + n + 1)
                    d16 = d[:, :].bitcast(BF16)
                    for t in range(NT):
                        mm = pe.transpose(d16[0:8, t * P:t * P + P],
                                          max_parts[:, t].rearrange("p a j x -> p (a j x)"), identb[:, :])
                    mm.then_inc(mt_ready, 1)
                elif name == "OT":
                    pe.wait_ge(o_copied, 8 * b + n + 1)
                    transpose_tiles(d, lambda t: o_sb[:, t * P:t * P + P], ident[:, :]).then_inc(ot_ready, 1)
                elif name == "AT":
                    pe.wait_ge(o_norm, 8 * b + 8)
                    transpose_tiles(d, lambda t: attn[:, t, n * P:n * P + P], ident[:, :]).then_inc(post_ready, 1)
                elif name == "OP":
                    pe.wait_ge(post_used, NPOST * b + POST_USED["AT", 1] + 1)
                    for t in range(2 * n, 2 * n + 2):
                        for c in range(EC):
                            for w, a in PASSES:
                                mm = pe.matmul(d[:, (t % 2) * E:(t % 2) * E + E], attn_parts[:, a, c, t * P:t * P + P],
                                               wo_parts[:, w, c, :], start=(c == 0 and (w, a) == PASSES[0]),
                                               stop=(c == EC - 1 and (w, a) == PASSES[-1]))
                    mm.then_inc(post_ready, 1)
                elif name == "X2T":
                    pe.wait_ge(ln_out[1], 4 * b + 4)
                    transpose_tiles(d, lambda t: x2n[:, t, n * P:n * P + P], ident[:, :]).then_inc(post_ready, 1)
                elif name in "AB":
                    pe.wait_ge(post_used, NPOST * b + POST_USED["X2T", 1] + 1)
                    for c in range(EC):
                        for part in range(2):
                            mm = pe.matmul(d[0:HB, :], t13[:, "AB".index(name), c, n * HB:n * HB + HB],
                                           x2T[:, part, c, :], start=(c == 0 and part == 0),
                                           stop=(c == EC - 1 and part == 1))
                    mm.then_inc(post_ready, 1)
                elif name == "DN":
                    for m in range(NB):
                        if n == 0:
                            pe.wait_ge(glo_done, NB * b + m + 1)
                        for part in range(2):
                            mm = pe.matmul(d[:, 0:E], gT[:, part, m, n * P:n * P + P], t2[:, m, :],
                                           start=(m == 0 and part == 0), stop=(m == NB - 1 and part == 1))
                    mm.then_inc(down_ready, 1)

            def iteration(i, att, pre, post, down):
                for t in range(8 * QUADS):
                    k, m = t // 8, t % 8
                    if att:
                        transposed_scores(i, k, m)
                    if k + 2 < QUADS and att:
                        scores(i, k + 2, m)
                    if k + 2 >= QUADS and pre:
                        scores(i + 1, k + 2 - QUADS, m)
                    if m in PV_SLOTS and (att if k else post):
                        values(*((i, k - 1) if k else (i - 1, QUADS - 1)), PV_SLOTS.index(m))
                    for cat, name, n in jobs_at(t, i):
                        if runs(cat, name, n, att, pre, post, down):
                            b, q = job_batch(cat, name, n, i)
                            dense(name, q, b)

            pe.wait_ge(ld_w["ident"], 16)
            pe.wait_ge(consts, 5)
            for c in range(EC):
                dense("X1T", c, 0)
            pe.wait_ge(qk_summed, 1)
            pe.matmul(s_bank[0][:, 0:1], ones[:, :], abs_sums[:, 5:6], start=True, stop=True).then_inc(qk_sum_ready, 1)
            for j in range(4):
                pe.wait_ge(qk_split, 2 if j < 2 else 4)
                dense("QK", j, 0)
            pe.wait_ge(abs_done, 6)
            pe.matmul(s_bank[1][:, 0:5], ones[:, :], abs_sums[:, 0:5], start=True, stop=True).then_inc(scale_ready, 1)
            pe.wait_ge(vo_split, 2)
            for h in range(2):
                dense("V", h, 0)
            pe.wait_ge(setup, 1)
            for m in range(SLOTS):
                scores(0, 0, m)
            dense("MT", 0, 0)
            for m in range(SLOTS):
                scores(0, 1, m)
            iteration(0, True, True, False, False)
            pe.wait_ge(vo_split, 4)
            pe.wait_ge(ternary, 3)
            iteration(1, True, True, True, False)
            with pe.Fori(*LOOP) as i:
                take_over(i)
                iteration(i, True, True, True, True)
            take_over(B - 1)
            iteration(B - 1, True, False, True, True)
            iteration(B, False, False, True, True)
            iteration(B + 1, False, False, False, True)

        @block.scalar
        def _(act):
            def exps(b, q, m):
                chunk, pair = m // 2, m % 2
                for j in range(2):
                    n = 2 * m + j
                    act.wait_ge(st_ready, 128 * b + 16 * q + n + 1)
                    act.activation(probs[:, q % 2, chunk, 2 * pair + j, :], st_bank[j][:, :], ACT.Exp,
                                   scale=SCALE).then_inc(exp_done, 1)

            def copy_x1T(b, c):
                act.wait_ge(pre_ready, NPRE * b + PRE_USED["X1T", c] + 1)
                act.copy(xhT[:, 0, c, :], d_bank[BANK["X1T", c]][:, :]).then_inc(xh_high, 1)

            def copy_raw(b, j):
                act.wait_ge(pre_ready, NPRE * b + PRE_USED["QK", j] + 1)
                if not isinstance(b, int) or b > 0:
                    act.wait_ge(rope_step, rope_count(b, 0))
                act.activation(raw[:, j, :], d_bank[BANK["QK", j]][:, :], ACT.Copy, scale=unscale[:, 2:3]).then_inc(pre_used, 1)

            def copy_v(b, h):
                act.wait_ge(pre_ready, NPRE * b + PRE_USED["V", h] + 1)
                wait(act, v_ready, 4 * b)
                act.activation(v_next[:, 2 * h:2 * h + 2, :, 0:VD],
                               d_bank[BANK["V", h]][:, :].rearrange("p (n h e) -> p n h e", n=2, h=H), ACT.Copy,
                               scale=unscale[:, 0:1]).then_inc(pre_used, 1)

            def move_v(b, c):
                act.wait_ge(pre_used, NPRE * b + NPRE)
                wait(act, pv_done, 32 * (b - 1) + 28 + c + 1)
                act.copy(v_sb[:, c], v_next[:, c]).then_inc(v_ready, 1)

            def copy_o(b, q):
                act.wait_ge(pv_done, 32 * b + 4 * q + 4)
                wait(act, ot_ready, 8 * b + q)
                act.copy(o_sb[:, :], o_bank[:, :]).then_inc(o_copied, 1)

            def copy_max_rows(b, q):
                act.wait_ge(mt_ready, 8 * b + q + 1)
                if q >= 2:
                    act.wait_ge(shift_loaded[q % 2], 256 * b + 64 * (q // 2))
                else:
                    wait(act, shift_loaded[q % 2], 256 * b)
                d16 = d_bank[BANK["MT", (q - 1) % 8]][:, :].bitcast(BF16)
                act.copy(max_rows[:, q % 2, :], d16[0:8, 0:T]).then_inc(mt_used, 1)

            def cast_part(b, n):
                side, part, a = n // 4, (n // 2) % 2, n % 2
                src = roped_even[:, side, :] if a == 0 else raw[:, 2 * side + 1, :]
                if n == 0:
                    wait(act, scr_written, 96 * b)
                if isinstance(b, int) and b == 0:
                    done, value = ((first_rope, 6), (rope_step, 2), (first_rope, 12), (first_rope, 14))[n // 2]
                    act.wait_ge(done, value)
                else:
                    act.wait_ge(rope_step, rope_count(b, (6, 8, 14, 18)[n // 2]))
                act.copy(parts[:, side, part, a, :], src).then_inc(cast_done, 1)

            def copy_attnT(b, c):
                act.wait_ge(post_ready, NPOST * b + POST_USED["AT", c] + 1)
                act.copy(attn_parts[:, 0, c, :], d_bank[BANK["AT", c]][:, :]).then_inc(attn_high, 1)

            def x2_high(b, c):
                act.wait_ge(post_ready, NPOST * b + POST_USED["X2T", c] + 1)
                act.copy(x2T[:, 0, c, :], job_bank("X2T", c, b)[:, :]).then_inc(x2h_done, 1)

            def tanh(b, m):
                act.wait_ge(post_ready, NPOST * b + POST_USED["A", m] + 1)
                if m >= 2:
                    act.wait_ge(post_used, NPOST * b + POST_USED["A", m - 2] + 1)
                act.activation(th[:, m % 2, :], job_bank("A", m, b)[0:HB, :], ACT.Tanh,
                               scale=half[0:HB, 0:1]).then_inc(tanh_done, 1)

            def g_high(b, m):
                act.wait_ge(post_used, NPOST * b + POST_USED["B", m] + 1)
                act.copy(gT[:, 0, m, :], g[:, m % 2, :]).then_inc(ghi_done, 1)

            def iteration(i, att, pre, post, down):
                for t in range(8 * QUADS):
                    k, m = t // 8, t % 8
                    if m == 3 and (att if k < 7 else pre):
                        copy_max_rows(*job_batch("att", "MT", k, i))
                    if m == 7 and (att if k else post):
                        copy_o(*((i, k - 1) if k else (i - 1, QUADS - 1)))
                    if att and k == 0 and m - 1 in PV_SLOTS:
                        move_v(i, PV_SLOTS.index(m - 1))
                    for cat, name, n in jobs_at(t - 1, i):
                        if not runs(cat, name, n, att, pre, post, down):
                            continue
                        if name == "X1T":
                            copy_x1T(i + 1, n)
                        elif name == "QK":
                            copy_raw(i + 1, n)
                        elif name == "V":
                            copy_v(i + 1, n)
                        elif name == "AT":
                            copy_attnT(i - 1, n)
                        elif name == "X2T":
                            x2_high(i - 1, n)
                        elif name == "A":
                            tanh(i - 1, n)
                    if att:
                        if t == SLOTS and isinstance(i, int) and i == 0:
                            act.wait_ge(ternary, 3)
                            act.wait_ge(vo_split, 4)
                        exps(i, k, m)
                    if pre:
                        for n in CAST_AT.get(t, ()):
                            cast_part(i + 1, n)
                    for cat, name, n in jobs_at(t - 1, i):
                        if name == "B" and post:
                            g_high(i - 1, n)

            act.wait_ge(lam_sum, 3)
            act.activation(lam_e[:, :], lam_s[:, :], ACT.Exp).then_inc(lam_exp, 1)
            for c in range(EC):
                copy_x1T(0, c)
            for j in range(4):
                copy_raw(0, j)
            act.wait_ge(consts, 5)
            for n in FIRST_CASTS:
                cast_part(0, n)
            for h in range(2):
                copy_v(0, h)
            copy_max_rows(0, 0)
            iteration(0, True, True, False, False)
            iteration(1, True, True, True, False)
            with act.Fori(*LOOP) as i:
                iteration(i, True, True, True, True)
            iteration(B - 1, True, False, True, True)
            iteration(B, False, False, True, True)
            iteration(B + 1, False, False, False, True)

        @block.vector
        def _(dve):
            def row_maxima(b, q, m):
                for j in range(2):
                    dve.wait_ge(s_ready, 128 * b + 16 * q + 2 * m + j + 1)
                    dve.tensor_reduce(row_max[:, q % 2, m // 2, m % 2, j:j + 1], s_bank[S_BANKS[16 * q + 2 * m + j]][:, :], AX.X,
                                      ALU.max).then_inc(s_used, 1)

            def split_max_high(b, q):
                dve.wait_ge(s_used, 128 * b + 16 * q + 16)
                wait(dve, mt_ready, 8 * b + q)
                dve.tensor_scalar(max_parts[:, :, :, :, 0], row_max[:, q % 2], -1.0, None,
                                  ALU.mult).then_inc(max_hi, 1)

            def split_max_low(b, q):
                dve.wait_ge(max_hi, 8 * b + q + 1)
                dve.scalar_tensor_tensor(out=max_parts[:, :, :, :, 1], in0=row_max[:, q % 2], scalar=-1.0,
                                         in1=max_parts[:, :, :, :, 0], op0=ALU.mult,
                                         op1=ALU.subtract).then_inc(max_split, 1)

            def o_view(q):
                return d_bank[BANK["OT", (q + 2) % 8]][:, :].rearrange("p (n s e) -> p n s e", n=NT, s=4)

            def out_recip(b, q):
                dve.wait_ge(ot_ready, 8 * b + q + 1)
                dve.reciprocal(o_recip[:, :, :], o_view(q)[:, :, :, VD]).then_inc(o_step, 1)

            def out_scale_heads(b, q):
                dve.wait_ge(o_step, 48 * b + 6 * q + 1)
                dve.tensor_tensor(o_scaled[:, :, :, :], o_view(q)[:, :, :, 0:VD],
                                  o_recip[:, :, :].unsqueeze(3).to_broadcast([P, NT, 4, VD]), ALU.mult).then_inc(ot_used, 1)

            def out_diff(b, q):
                dve.wait_ge(ot_used, 8 * b + q + 1)
                if q == 0 and isinstance(b, int) and b == 0:
                    dve.wait_ge(lam_done, 2)
                v = o_scaled[:, :, :, :].rearrange("p n (a j) e -> p n a j e", j=2)
                dve.scalar_tensor_tensor(out=o_diff[:, :, :, :], in0=v[:, :, :, 1], scalar=neg_lam[:, 0:1],
                                         in1=v[:, :, :, 0], op0=ALU.mult, op1=ALU.add).then_inc(o_step, 1)

            def out_clamp(b, q):
                dve.wait_ge(o_step, 48 * b + 6 * q + 2)
                dve.tensor_scalar(o_sq[:, :, :, :], o_diff[:, :, :, :], SQUARE_MAX, -SQUARE_MAX, ALU.min,
                                  ALU.max).then_inc(o_step, 1)

            def out_square(b, q):
                dve.wait_ge(o_step, 48 * b + 6 * q + 3)
                dve.scalar_tensor_tensor(out=o_sq[:, :, :, :], in0=o_sq[:, :, :, :], scalar=1.0 / VD,
                                         in1=o_sq[:, :, :, :], op0=ALU.mult, op1=ALU.mult).then_inc(o_step, 1)

            def out_sum(b, q):
                dve.wait_ge(o_step, 48 * b + 6 * q + 4)
                dve.tensor_reduce(o_ss[:, :], o_sq[:, :, :, :].rearrange("p n a e -> p (n a) e"), AX.X,
                                  ALU.add).then_inc(o_step, 1)

            def out_eps(b, q):
                dve.wait_ge(o_step, 48 * b + 6 * q + 5)
                dve.tensor_scalar(o_ms[:, :], o_ss[:, :], EPS, None, ALU.add).then_inc(o_step, 1)

            def out_mask(b, q):
                dve.wait_ge(o_rms_done, 8 * b + q + 1)
                dve.scalar_tensor_tensor(out=o_rms_in[:, :], in0=o_ms[:, :], scalar=MEAN_MAX, in1=o_rms[:, :],
                                         op0=ALU.is_lt, op1=ALU.mult).then_inc(o_masked, 1)

            def out_norm(b, q):
                dve.wait_ge(o_masked, 8 * b + q + 1)
                if q == 0:
                    wait(dve, post_ready, NPOST * (b - 1) + POST_USED["AT", 1] + 1)
                dve.tensor_tensor(attn[:, :, q * 2 * VD:(q + 1) * 2 * VD].rearrange("p n (a e) -> p n a e", a=2),
                                  o_diff[:, :, :, :],
                                  o_rms_in[:, :].rearrange("p (n a) -> p n a", a=2).unsqueeze(3).to_broadcast([P, NT, 2, VD]),
                                  ALU.mult).then_inc(o_norm, 1)

            def ln_stats(s, src, b, tiles=range(NT)):
                for n in tiles:
                    dve.bn_stats(stats[s][:, n, :], src[:, n, :]).then_inc(ln_step[s], 1)

            def ln_stats_written(s, b):
                dve.wait_ge(ln_step[s], 9 * b + 4)

            def ln_aggregate(s, b):
                for n in range(NT):
                    dve.bn_aggr(mean_var[s][:, n, :], stats[s][:, n, :]).then_inc(ln_step[s], 1)

            def ln_variance(s, b):
                dve.wait_ge(ln_step[s], 9 * b + 8)
                dve.tensor_scalar(var_eps[s][:, :], mean_var[s][:, :, 1], EPS, None, ALU.add).then_inc(ln_step[s], 1)

            def ln_apply(s, src, dst, b, tiles=range(NT)):
                if tiles[0] == 0:
                    dve.wait_ge(ln_rstd[s], b + 1)
                if s == 0 and tiles[0] == 0:
                    wait(dve, pre_ready, NPRE * (b - 1) + 2)
                    wait(dve, glo_done, NB * (b - 2))
                for n in tiles:
                    dve.tensor_scalar(dst[:, n, :], src[:, n, :], mean_var[s][:, n, 0:1], rstd[s][:, n:n + 1],
                                      ALU.subtract, ALU.mult).then_inc(ln_out[s], 1)

            def xh_low(b, c):
                dve.wait_ge(xh_high, 2 * b + c + 1)
                dve.tensor_tensor(xhT[:, 1, c, :], d_bank[BANK["X1T", c]][:, :], xhT[:, 0, c, :],
                                  ALU.subtract).then_inc(pre_used, 1)

            def attn_low(b, c):
                dve.wait_ge(attn_high, 2 * b + c + 1)
                dve.tensor_tensor(attn_parts[:, 1, c, :], d_bank[BANK["AT", c]][:, :], attn_parts[:, 0, c, :],
                                  ALU.subtract).then_inc(post_used, 1)

            def residual(b, h):
                dve.wait_ge(post_ready, NPOST * b + POST_USED["OP", h] + 1)
                if h == 0:
                    dve.wait_ge(ld_xres, 16 * b + 16)
                    wait(dve, out_stored, 16 * b)
                dve.scalar_tensor_tensor(out=x2[:, 2 * h:2 * h + 2, :],
                                         in0=d_bank[BANK["OP", h]][:, :].rearrange("p (n e) -> p n e", n=2),
                                         scalar=unscale[:, 1:2], in1=x_res[:, 2 * h:2 * h + 2, :], op0=ALU.mult,
                                         op1=ALU.add).then_inc(post_used, 1)

            def x2_low(b, c):
                dve.wait_ge(x2h_done, 2 * b + c + 1)
                dve.tensor_tensor(x2T[:, 1, c, :], job_bank("X2T", c, b)[:, :], x2T[:, 0, c, :],
                                  ALU.subtract).then_inc(post_used, 1)

            def gate_a(b, m):
                dve.wait_ge(post_used, NPOST * b + POST_USED["A", m])
                dve.wait_ge(tanh_done, NB * b + m + 1)
                dve.scalar_tensor_tensor(out=gate[:, :], in0=th[:, m % 2, :], scalar=1.0,
                                         in1=job_bank("A", m, b)[0:HB, :], op0=ALU.add,
                                         op1=ALU.mult).then_inc(post_used, 1)

            def gate_b(b, m):
                dve.wait_ge(post_used, NPOST * b + POST_USED["A", m] + 1)
                dve.wait_ge(post_ready, NPOST * b + POST_USED["B", m] + 1)
                wait(dve, glo_done, NB * b + max(m - 1, 0))
                dve.scalar_tensor_tensor(out=g[:, m % 2, :], in0=gate[:, :], scalar=0.125,
                                         in1=job_bank("B", m, b)[0:HB, :], op0=ALU.mult,
                                         op1=ALU.mult).then_inc(post_used, 1)

            def finish(b, n):
                dve.wait_ge(down_ready, NT * b + n + 1)
                dve.scalar_tensor_tensor(out=x2[:, n, :], in0=d_bank[BANK["DN", n]][:, 0:E], scalar=out_scale[:, 0:1],
                                         in1=x2[:, n, :], op0=ALU.mult, op1=ALU.add).then_inc(down_used, 1)

            def iteration(i, att, pre, post, down):
                for t in range(8 * QUADS):
                    k, m = t // 8, t % 8
                    if att if k < 7 else pre:
                        b, q = job_batch("att", "MT", k, i)
                        if m == 0:
                            split_max_high(b, q)
                        if m == 1:
                            split_max_low(b, q)
                    if m in (1, 2) and (att if k >= 3 else post):
                        (out_mask, out_norm)[m - 1](*((i, k - 3) if k >= 3 else (i - 1, k + 5)))
                    if att if k >= 2 else post:
                        b, q = job_batch("att", "OT", k, i)
                        for at, step in ((2, out_recip), (2, out_scale_heads), (4, out_diff), (5, out_clamp),
                                         (6, out_square), (6, out_sum), (7, out_eps)):
                            if m == at:
                                step(b, q)
                    if pre:
                        if t == LN1_AT[0]:
                            dve.wait_ge(ld_x, 16 * (i + 1) + 16)
                        if LN1_AT[0] <= t < LN1_AT[0] + 2:
                            ln_stats(0, x_pre, i + 1, [2 * (t - LN1_AT[0]), 2 * (t - LN1_AT[0]) + 1])
                        if t == LN1_AT[1]:
                            ln_aggregate(0, i + 1)
                        if t == LN1_AT[2]:
                            ln_variance(0, i + 1)
                        if LN1_AT[3] <= t < LN1_AT[3] + 2:
                            ln_apply(0, x_pre, x1n, i + 1, [2 * (t - LN1_AT[3]), 2 * (t - LN1_AT[3]) + 1])
                        for cat, name, n in jobs_at(t - X1T_LAG, i):
                            if name == "X1T":
                                xh_low(i + 1, n)
                    if post:
                        for cat, name, n in jobs_at(t - AT_LAG, i):
                            if name == "AT":
                                attn_low(i - 1, n)
                        for h in range(2):
                            if t == OP_AT[h] + 1:
                                residual(i - 1, h)
                            if t == OP_AT[h] + 2:
                                dve.wait_ge(post_used, NPOST * (i - 1) + POST_USED["OP", h] + 1)
                                ln_stats(1, x2, i - 1, [2 * h, 2 * h + 1])
                        if t == LN2_AT[1]:
                            ln_aggregate(1, i - 1)
                        if t == LN2_AT[2]:
                            ln_variance(1, i - 1)
                        if LN2_AT[3] <= t < LN2_AT[3] + 2:
                            ln_apply(1, x2, x2n, i - 1, [2 * (t - LN2_AT[3]), 2 * (t - LN2_AT[3]) + 1])
                        for cat, name, n in jobs_at(t - 2, i):
                            if name == "X2T":
                                x2_low(i - 1, n)
                            if name == "A":
                                gate_a(i - 1, n)
                        for cat, name, n in jobs_at(t - 1, i):
                            if name == "B":
                                gate_b(i - 1, n)
                    if down:
                        for cat, name, n in jobs_at(t - 1, i):
                            if name == "DN":
                                finish(i - 2, n)
                    if t == LN1_AT[1] - 1 and pre:
                        ln_stats_written(0, i + 1)
                    if t == LN2_AT[1] - 1 and post:
                        ln_stats_written(1, i - 1)
                    if k + 2 < QUADS and att:
                        row_maxima(i, k + 2, m)
                    if k + 2 >= QUADS and pre:
                        row_maxima(i + 1, k + 2 - QUADS, m)

            dve.memset(ones[:, :], 1.0).then_inc(consts, 1)
            dve.memset(minus_half[:, :], -0.5).then_inc(consts, 1)
            dve.memset(v_next[:, :, :, VD:VD + 1], 1.0).then_inc(consts, 1)
            dve.memset(o_bank[:, :], 0.0).then_inc(consts, 1)
            dve.memset(abs_sums[:, 0:5], 0.0).then_inc(abs_done, 1)
            dve.wait_ge(ld_w["ident"], 16)
            dve.tensor_copy(identb[:, :], ident[:, :]).then_inc(consts, 1)
            dve.wait_ge(ld_x, 16)
            ln_stats(0, x_pre, 0)
            ln_stats_written(0, 0)
            ln_aggregate(0, 0)
            ln_variance(0, 0)
            dve.wait_ge(ld_w["small"], 32)
            dve.tensor_tensor(lam_p[:, 0], lam_v[:, 0], lam_v[:, 1], ALU.mult).then_inc(lam_sum, 1)
            ln_apply(0, x_pre, x1n, 0)
            dve.tensor_tensor(lam_p[:, 1], lam_v[:, 2], lam_v[:, 3], ALU.mult).then_inc(lam_sum, 1)
            dve.wait_ge(lam_sum, 2)
            dve.tensor_reduce(lam_s[:, :], lam_p[:, :, :], AX.X, ALU.add).then_inc(lam_sum, 1)
            def split_high(rawv, high, n, done):
                dve.tensor_scalar(high, rawv, upscale[:, n:n + 1], None, ALU.mult).then_inc(done, 1)

            def split_low(rawv, high, low, n, done):
                dve.scalar_tensor_tensor(out=low, in0=rawv, scalar=upscale[:, n:n + 1], in1=high, op0=ALU.mult,
                                         op1=ALU.subtract).then_inc(done, 1)

            dve.wait_ge(ld_w["qk"], 16)
            dve.tensor_reduce(abs_sums[:, 5:6], wqk_raw.rearrange("p c j m -> p (c j m)"), AX.X, ALU.add,
                              apply_absolute_value=True).then_inc(qk_summed, 1)
            for c in range(EC):
                xh_low(0, c)
            dve.wait_ge(qk_sum_ready, 1)
            dve.tensor_scalar(unscale[:, 2:3], s_bank[0][:, 0:1], 1.0 / HALF_SUM, FLOOR, ALU.mult, ALU.max).then_inc(qk_unit, 1)
            dve.wait_ge(qk_unit, 1)
            dve.reciprocal(upscale[:, 2:3], unscale[:, 2:3]).then_inc(qk_unit, 1)
            dve.wait_ge(qk_unit, 2)
            for side in range(2):
                rawv, high, low = (v[:, :, 2 * side:2 * side + 2, :] for v in (wqk_raw, wqk_parts[:, 0], wqk_parts[:, 1]))
                split_high(rawv, high, 2, qk_split)
                dve.wait_ge(qk_split, 2 * side + 1)
                split_low(rawv, high, low, 2, qk_split)
            dve.wait_ge(ld_w["vo"], 32)
            for c in range(EC):
                dve.tensor_scalar(wo_raw[:, c, :], wo_raw[:, c, :], gcol[:, 0:1], 1.0 - LAMBDA_INIT, ALU.mult,
                                  ALU.mult).then_inc(wo_scaled, 1)
            dve.wait_ge(abs_done, 1)
            dve.tensor_reduce(abs_sums[:, 3:4], wv_raw.rearrange("p c e -> p (c e)"), AX.X, ALU.add,
                              apply_absolute_value=True).then_inc(abs_done, 1)
            dve.wait_ge(wo_scaled, 2)
            dve.tensor_reduce(abs_sums[:, 4:5], wo_raw.rearrange("p c e -> p (c e)"), AX.X, ALU.add,
                              apply_absolute_value=True).then_inc(abs_done, 1)
            dve.wait_ge(ld_w["tern"], 48)
            for w in range(2):
                dve.tensor_reduce(abs_sums[:, w:w + 1], w13_raw[:, w].rearrange("p c h -> p (c h)"), AX.X, ALU.add,
                                  apply_absolute_value=True).then_inc(abs_done, 1)
            dve.tensor_reduce(abs_sums[0:HB, 2:3], w2_raw.rearrange("p m e -> p (m e)"), AX.X, ALU.add,
                              apply_absolute_value=True).then_inc(abs_done, 1)
            dve.wait_ge(ld_w["rope"], 16)
            cos, sin = cos_sin[:, 0, :], cos_sin[:, 1, :]
            for side, room in enumerate((x2, x_res)):
                even, odd, rot = raw[:, 2 * side, :], raw[:, 2 * side + 1, :], roped_even[:, side, :]
                odd_sin, even_sin = (room[:, 2 * n:2 * n + 2, :].rearrange("p n e -> p (n e)") for n in range(2))
                dve.wait_ge(pre_used, PRE_USED["QK", 2 * side] + 1)
                dve.tensor_tensor(rot, even, cos, ALU.mult).then_inc(first_rope, 1)
                dve.tensor_tensor(even_sin, even, sin, ALU.mult).then_inc(first_rope, 1)
                dve.wait_ge(pre_used, PRE_USED["QK", 2 * side + 1] + 1)
                dve.tensor_tensor(odd_sin, odd, sin, ALU.mult).then_inc(first_rope, 1)
                dve.wait_ge(first_rope, 6 * side + 3)
                dve.tensor_tensor(odd, odd, cos, ALU.mult).then_inc(first_rope, 1)
                dve.tensor_tensor(rot, rot, odd_sin, ALU.subtract).then_inc(first_rope, 1)
                dve.wait_ge(first_rope, 6 * side + 4)
                dve.tensor_tensor(odd, even_sin, odd, ALU.add).then_inc(first_rope, 1)
            for n in range(4, 8):
                v = roped_even[:, 1, :] if n % 2 == 0 else raw[:, 3, :]
                dve.wait_ge(cast_done, FIRST_CASTS.index(n) + 1)
                dst = v if n < 6 else parts[:, 1, 2, n % 2, :]
                dve.tensor_tensor(dst, v, parts[:, 1, (n - 4) // 2, n % 2, :], ALU.subtract).then_inc(first_rope, 1)
            dve.wait_ge(scale_ready, 1)
            dve.tensor_scalar(unscale[:, 0:2], s_bank[1][:, 3:5], 1.0 / HALF_SUM, FLOOR, ALU.mult, ALU.max).then_inc(vo_unit, 1)
            dve.wait_ge(vo_unit, 1)
            dve.reciprocal(upscale[:, 0:2], unscale[:, 0:2]).then_inc(vo_unit, 1)
            dve.wait_ge(vo_unit, 2)
            split_high(wv_raw, wv_parts[:, 0], 0, vo_split)
            dve.wait_ge(vo_split, 1)
            split_low(wv_raw, wv_parts[:, 0], wv_parts[:, 1], 0, vo_split)
            dve.wait_ge(lam_exp, 1)
            dve.tensor_scalar(neg_lam[:, :], lam_e[:, 1:2], -LAMBDA_INIT, None, ALU.add).then_inc(lam_done, 1)
            dve.wait_ge(lam_done, 1)
            dve.tensor_tensor(neg_lam[:, :], neg_lam[:, :], lam_e[:, 0:1], ALU.subtract).then_inc(lam_done, 1)
            dve.tensor_scalar(scales[:, :], s_bank[1][:, 0:3], 1.0 / (HIDDEN * E), None, ALU.mult).then_inc(setup, 1)
            dve.wait_ge(setup, 1)
            dve.tensor_scalar(half[:, :], scales[:, :], 0.5, None, ALU.mult).then_inc(setup, 1)
            dve.tensor_scalar(neg_half[:, :], scales[:, :], -0.5, None, ALU.mult).then_inc(setup, 1)
            dve.tensor_tensor(s13[:, :], scales[:, 0:1], scales[:, 1:2], ALU.mult).then_inc(setup, 1)
            dve.wait_ge(setup, 4)
            dve.scalar_tensor_tensor(out=out_scale[:, :], in0=s13[:, :], scalar=4.0, in1=scales[:, 2:3],
                                     op0=ALU.mult, op1=ALU.mult).then_inc(setup, 1)
            for w, (rawv, dst) in enumerate(((w13_raw[:, 0].rearrange("p c h -> p (c h)"), t13[:, 0].rearrange("p c h -> p (c h)")),
                                             (w13_raw[:, 1].rearrange("p c h -> p (c h)"), t13[:, 1].rearrange("p c h -> p (c h)")),
                                             (w2_raw.rearrange("p m e -> p (m e)"), t2[:, :, :].rearrange("p m e -> p (m e)")))):
                rows, n = rawv.shape
                wait(dve, ternary, w)
                dve.tensor_scalar(below[0:rows, 0:n], rawv, neg_half[0:rows, w:w + 1], None, ALU.is_lt).then_inc(setup, 1)
                dve.wait_ge(setup, 6 + w)
                dve.scalar_tensor_tensor(out=dst, in0=rawv, scalar=half[0:rows, w:w + 1], in1=below[0:rows, 0:n],
                                         op0=ALU.is_gt, op1=ALU.subtract).then_inc(ternary, 1)
            split_high(wo_raw, wo_parts[:, 0], 1, vo_split)
            dve.wait_ge(vo_split, 3)
            split_low(wo_raw, wo_parts[:, 0], wo_parts[:, 1], 1, vo_split)
            for m in range(SLOTS):
                row_maxima(0, 0, m)
            split_max_high(0, 0)
            split_max_low(0, 0)
            for m in range(SLOTS):
                row_maxima(0, 1, m)
            iteration(0, True, True, False, False)
            iteration(1, True, True, True, False)
            with dve.Fori(*LOOP) as i:
                iteration(i, True, True, True, True)
            iteration(B - 1, True, False, True, True)
            iteration(B, False, False, True, True)
            iteration(B + 1, False, False, False, True)

        @block.gpsimd
        def _(pool):
            def rope_ops(b, first, last):
                for n in range(first, last):
                    pool.wait_ge(rope_step, rope_count(b, n))
                    rotate_and_split(b, n)

            def rotate_and_split(b, n):
                cos, sin = cos_sin[:, 0, :], cos_sin[:, 1, :]
                for side, base in ((0, 0), (1, 8)):
                    even, odd, rot = raw[:, 2 * side, :], raw[:, 2 * side + 1, :], roped_even[:, side, :]
                    if n == base:
                        pool.wait_ge(pre_used, NPRE * b + PRE_USED["QK", 2 * side + 1] + 1)
                        return pool.tensor_tensor(rot, even, cos, ALU.mult).then_inc(rope_step, 1)
                    if n == base + 1:
                        return pool.tensor_tensor(rope_tmp[:, :], odd, sin, ALU.mult).then_inc(rope_step, 1)
                    if n == base + 2:
                        return pool.tensor_tensor(rot, rot, rope_tmp[:, :], ALU.subtract).then_inc(rope_step, 1)
                    if n == base + 3:
                        return pool.tensor_tensor(even, even, sin, ALU.mult).then_inc(rope_step, 1)
                    if n == base + 4:
                        return pool.tensor_tensor(odd, odd, cos, ALU.mult).then_inc(rope_step, 1)
                    if n == base + 5:
                        return pool.tensor_tensor(odd, even, odd, ALU.add).then_inc(rope_step, 1)
                side = 0 if n in (6, 7, 14, 15) else 1
                part = 0 if n in (6, 7, 16, 17) else 1
                a = n % 2
                v = roped_even[:, side, :] if a == 0 else raw[:, 2 * side + 1, :]
                pool.wait_ge(cast_done, CASTS * b + 4 * side + 2 * part + a + 1)
                dst = v if part == 0 else parts[:, side, 2, a, :]
                pool.tensor_tensor(dst, v, parts[:, side, part, a, :], ALU.subtract).then_inc(rope_step, 1)

            def ln_power(s, b):
                pool.wait_ge(ln_step[s], 9 * b + 9)
                pool.tensor_tensor(rstd[s][:, :], var_eps[s][:, :], minus_half[:, 0:NT], ALU.pow).then_inc(ln_rstd[s], 1)

            def out_power(b, q):
                pool.wait_ge(o_step, 48 * b + 6 * q + 6)
                wait(pool, o_masked, 8 * b + q)
                pool.tensor_tensor(o_rms[:, :], o_ms[:, :], minus_half[:, :], ALU.pow).then_inc(o_rms_done, 1)

            def g_low(b, m):
                pool.wait_ge(ghi_done, NB * b + m + 1)
                pool.tensor_tensor(gT[:, 1, m, :], g[:, m % 2, :], gT[:, 0, m, :], ALU.subtract).then_inc(glo_done, 1)

            def iteration(i, att, pre, post, down):
                for t in range(8 * QUADS):
                    k = t // 8
                    if pre and t == LN1_AT[2]:
                        ln_power(0, i + 1)
                    if pre and t in ROPE_AT:
                        rope_ops(i + 1, *ROPE_AT[t])
                    if post and t == LN2_AT[2]:
                        ln_power(1, i - 1)
                    for cat, name, n in jobs_at(t - 2, i):
                        if name == "B" and post:
                            g_low(i - 1, n)
                    if t % 8 == 7 and (att if k >= 2 else post):
                        out_power(*job_batch("att", "OT", k, i))

            pool.wait_ge(consts, 5)
            ln_power(0, 0)
            for n in range(4):
                a = n % 2
                v = roped_even[:, 0, :] if a == 0 else raw[:, 1, :]
                pool.wait_ge(cast_done, FIRST_CASTS.index(n) + 1)
                dst = v if n < 2 else parts[:, 0, 2, a, :]
                pool.tensor_tensor(dst, v, parts[:, 0, n // 2, a, :], ALU.subtract).then_inc(rope_step, 1)
            iteration(0, True, True, False, False)
            iteration(1, True, True, True, False)
            with pool.Fori(*LOOP) as i:
                iteration(i, True, True, True, True)
            iteration(B - 1, True, False, True, True)
            iteration(B, False, False, True, True)
            iteration(B + 1, False, False, False, True)


def rope_tables():
    angle = (1.0 / np.float32(1250) ** np.linspace(0.0, 1.0, HD // 2, dtype=np.float32)).astype(np.float32)
    freqs = np.arange(T, dtype=np.float32)[:, None] * angle
    rows = np.tile(freqs.T, (2 * H, 1)).astype(np.float32)
    return np.stack([np.cos(rows), np.sin(rows)]).astype(np.float32)


def kernel(**inputs):
    import ml_dtypes
    import concourse.bacc as bacc
    from concourse.bass_utils import run_bass_kernel_spmd

    a = {k: np.asarray(v) for k, v in inputs.items()}

    def rotary_pairs(w):
        return w.reshape(2 * H, HD // 2, 2, E).transpose(3, 2, 0, 1).reshape(E, 2, P)

    def pad_hidden(w):
        return np.concatenate([w, np.zeros((HPAD - HIDDEN,) + w.shape[1:], w.dtype)])

    pads = np.zeros((2, HD // 2, BLOCK - SHIFT_ROW, T), ml_dtypes.bfloat16)
    pads[1, 0, 0:2] = 1
    pads = pads.reshape(2, HD // 2, -1)
    arrays = {
        "x": a["L0_attn_x"],
        "wqk": np.concatenate([rotary_pairs(a["L0_attn_Wq"]), rotary_pairs(a["L0_attn_Wk"])], axis=1),
        "wv": a["L0_attn_Wv"].T, "wo": a["L0_attn_Wo"].T,
        "w1": pad_hidden(a["L0_ffn_w1"]).T, "w3": pad_hidden(a["L0_ffn_w3"]).T, "w2": pad_hidden(a["L0_ffn_w2"].T),
        "rope": rope_tables(), "ident": np.eye(P, dtype=np.float32), "pads": pads,
        "lam": np.stack([a["L0_attn_lambda_q1"], a["L0_attn_lambda_k1"], a["L0_attn_lambda_q2"], a["L0_attn_lambda_k2"]]),
        "gamma": np.tile(a["L0_attn_gamma"], P // VD).reshape(P, 1),
    }
    arrays = {f"in_{k}": np.ascontiguousarray(v) for k, v in arrays.items()}
    nc = bacc.Bacc("TRN2", target_bir_lowering=False, num_devices=1)
    args = [nc.dram_tensor(k, v.shape, mybir.dt.from_np(v.dtype), kind="ExternalInput").ap() for k, v in arrays.items()]
    out = nc.dram_tensor("out", (B, T, E), F32, kind="ExternalOutput").ap()
    build(nc, *args, out)
    r = run_bass_kernel_spmd(nc, [arrays], core_ids=[0])
    return r.results[0]["out"]
```
